# Optimizing a Trainium2 kernel written in Bass

```python
import numpy as np
import jax
import jax.numpy as jnp

def _softmax(x, axis=-1):
    return jax.nn.softmax(x, axis=axis)

def _gelu(x):
    return jax.nn.gelu(x, approximate=True)

def _silu(x):
    return jax.nn.silu(x)

def _sigmoid(x):
    return jax.nn.sigmoid(x)

def _layernorm(x, axis=-1, eps=1e-05):
    m = jnp.mean(x, axis=axis, keepdims=True)
    v = jnp.var(x, axis=axis, keepdims=True)
    return (x - m) / jnp.sqrt(v + eps)

def _scatter_add(tgt, idx, src, axis=0):
    return tgt.at[idx].add(src)

def _segment_sum(src, seg, n):
    return jax.ops.segment_sum(src, seg, n)
kernel_name = 'mk_gnn_preln_d2_gnn_r8_74a6dc'

def setup_inputs(seed: int=0):
    np.random.seed(seed)
    _w = jnp.asarray

    def _rec_inputs():
        import jax
        import jax.numpy as jnp
        _gk = jax.random.key(seed)
        x = -0.0003713 + 1 * jax.random.normal(jax.random.fold_in(_gk, 1), (12500, 128), jnp.float32)
        src = jax.random.randint(jax.random.fold_in(_gk, 2), (200000,), 0, 12500, jnp.int32)
        dst = jax.random.randint(jax.random.fold_in(_gk, 3), (200000,), 0, 12500, jnp.int32)
        _o = jnp.argsort(dst, stable=True)
        src = src[_o]
        dst = dst[_o]
        edge_attr_128 = -6.47781e-05 + 0.999943 * jax.random.normal(jax.random.fold_in(_gk, 12), (200000, 128), jnp.float32)
        edge_weight = jax.random.uniform(jax.random.fold_in(_gk, 14), (200000,), jnp.float32, 0.0, 1)
        return (x, src, dst, edge_attr_128, edge_weight)
    x, src, dst, edge_attr_128, edge_weight = _rec_inputs()

    def _L0_gnn_setup():
        import jax, jax.numpy as jnp
        import numpy as np
        LN_EPS = 1e-05
        key = jax.random.key(seed)
        ks = jax.random.split(key, 10)
        N, E, D = (12500, 200000, 128)
        node_feats = jax.random.normal(ks[0], (N, D), dtype=jnp.float32)
        edge_feats = jax.random.normal(ks[1], (E, D), dtype=jnp.float32)
        edge_index = jax.random.randint(ks[2], (2, E), 0, N, dtype=jnp.int64)
        s1 = 1.0 / np.sqrt(D)
        s2 = 1.0 / np.sqrt(2 * D)
        W1 = jax.random.uniform(ks[3], (D, 2 * D), jnp.float32, -s1, s1)
        b1 = jax.random.uniform(ks[4], (2 * D,), jnp.float32, -s1, s1)
        gamma = jnp.ones((2 * D,), jnp.float32)
        beta = jnp.zeros((2 * D,), jnp.float32)
        W2 = jax.random.uniform(ks[5], (2 * D, D), jnp.float32, -s2, s2)
        b2 = jax.random.uniform(ks[6], (D,), jnp.float32, -s2, s2)
        eps = jnp.zeros((1,), jnp.float32)
        return {'node_feats': node_feats, 'edge_feats': edge_feats, 'edge_index': edge_index, 'num_nodes': N, 'eps': eps, 'W1': W1, 'b1': b1, 'gamma': gamma, 'beta': beta, 'W2': W2, 'b2': b2}
    _L0_gnn_all = _L0_gnn_setup()
    _L0_gnn_in = {k: v for k, v in _L0_gnn_all.items() if k in ('eps', 'W1', 'b1', 'gamma', 'beta', 'W2', 'b2')}
    del _L0_gnn_all

    def _L1_gnn_setup():
        import jax, jax.numpy as jnp
        import numpy as np
        N_NODES = 12500
        N_EDGES = 75000
        D_FEAT = 128
        key = jax.random.key(seed)
        k1, k2, k3, k4 = jax.random.split(key, 4)
        features = jax.random.normal(k1, (N_NODES, D_FEAT), dtype=jnp.float32)
        edge_weight = jax.random.uniform(k2, (N_EDGES,), dtype=jnp.float32)
        edge_src = jax.random.randint(k3, (N_EDGES,), 0, N_NODES)
        edge_dst = jax.random.randint(k4, (N_EDGES,), 0, N_NODES)
        return {'features': features, 'edge_weight': edge_weight, 'edge_src': edge_src, 'edge_dst': edge_dst}
    _L1_gnn_all = _L1_gnn_setup()
    _L1_gnn_in = {k: v for k, v in _L1_gnn_all.items() if k in ()}
    del _L1_gnn_all
    return {'x': x, 'src': src, 'dst': dst, 'edge_attr_128': edge_attr_128, 'edge_weight': edge_weight, 'L0_gnn_eps': _L0_gnn_in['eps'], 'L0_gnn_W1': _L0_gnn_in['W1'], 'L0_gnn_b1': _L0_gnn_in['b1'], 'L0_gnn_gamma': _L0_gnn_in['gamma'], 'L0_gnn_beta': _L0_gnn_in['beta'], 'L0_gnn_W2': _L0_gnn_in['W2'], 'L0_gnn_b2': _L0_gnn_in['b2']}

def reference(x, src, dst, edge_attr_128, edge_weight, L0_gnn_eps, L0_gnn_W1, L0_gnn_b1, L0_gnn_gamma, L0_gnn_beta, L0_gnn_W2, L0_gnn_b2):
    import jax
    import jax.numpy as jnp

    def _L0_gnn_ref(node_feats, edge_feats, edge_index, num_nodes, eps, W1, b1, gamma, beta, W2, b2):
        import jax, jax.numpy as jnp
        import numpy as np
        LN_EPS = 1e-05
        message = jax.nn.relu(node_feats[edge_index[1]] + edge_feats)
        message_reduce = jax.ops.segment_sum(message, edge_index[0], num_segments=num_nodes)
        h = (1.0 + eps) * node_feats + message_reduce
        h1 = h @ W1 + b1
        mu = jnp.mean(h1, axis=-1, keepdims=True)
        var = jnp.mean(jnp.square(h1 - mu), axis=-1, keepdims=True)
        h1 = (h1 - mu) * jax.lax.rsqrt(var + LN_EPS) * gamma + beta
        return jax.nn.relu(h1) @ W2 + b2

    def _L1_gnn_ref(features, edge_weight, edge_src, edge_dst):
        import jax, jax.numpy as jnp
        import numpy as np
        N_NODES = 12500
        N_EDGES = 75000
        D_FEAT = 128
        "Weighted neighbor sum: out[v] = sum_{(u->v)} w_uv * features[u];\n            nodes with no incoming edges keep their own feature (matches the\n            torch loop's isolated-node branch)."
        n = features.shape[0]
        msgs = edge_weight[:, None] * features[edge_src]
        agg = jax.ops.segment_sum(msgs, edge_dst, num_segments=n)
        deg = jax.ops.segment_sum(jnp.ones_like(edge_weight), edge_dst, num_segments=n)
        return jnp.where(deg[:, None] > 0, agg, features)
    edge_index = jnp.stack([src, dst])
    h = jnp.maximum(_layernorm(x, axis=-1), 0.0)
    x = x + _L0_gnn_ref(h, edge_attr_128, edge_index, 12500, L0_gnn_eps, L0_gnn_W1, L0_gnn_b1, L0_gnn_gamma, L0_gnn_beta, L0_gnn_W2, L0_gnn_b2)
    h = jnp.maximum(_layernorm(x, axis=-1), 0.0)
    x = x + _L1_gnn_ref(h, edge_weight, src, dst)
    return x

_drawn_inputs = setup_inputs


def setup_inputs(seed=0):
    import zlib

    import numpy as np

    out = dict(_drawn_inputs(seed))
    spreads = {'L0_gnn_gamma': (1.0, 0.2), 'L0_gnn_beta': (0.0, 0.1)}
    factors = {'L0_gnn_b1': 8.0}
    for name, (base, spread) in spreads.items():
        noise = np.random.default_rng([zlib.crc32(name.encode()), seed]).standard_normal(out[name].shape)
        drawn = base * np.exp(spread * noise) if base else spread * noise
        out[name] = jnp.asarray(drawn.astype(out[name].dtype))
    for name, factor in factors.items():
        out[name] = (out[name] * factor).astype(out[name].dtype)
    return out
```

```python
from contextlib import ExitStack

import concourse.bass as bass
from concourse import mybir

P = 128
D = 128
H = 256
TILES = 4
SUPER = P * TILES
SUPERS = 4
GROUP = SUPER * SUPERS
WIN = 64
CHUNK = 7
LN_EPS = 1e-5

ALU = mybir.AluOpType
ACT = mybir.ActivationFunctionType
AX_X = mybir.AxisListType.X
F32 = mybir.dt.float32
BF16 = mybir.dt.bfloat16
I32 = mybir.dt.int32


def build(nc, x, src, dst, edge_attr, edge_weight, eps, W1, b1, gamma, beta, W2, b2, out):
    N = x.shape[0]
    E = src.shape[0]
    NJ = -(-N // P)
    NP = NJ * P
    full_parts, rest_nodes = N // NJ, N % NJ
    DUMP = NP
    chunks = NJ // CHUNK
    assert NJ % (2 * CHUNK) == 0 and chunks >= 2
    windows = -(-N // WIN)
    G = E // GROUP
    rest = E % GROUP
    assert G >= 2 and rest % TILES == 0 and rest
    tail = [P] * (rest // SUPER) + ([rest % SUPER // TILES] if rest % SUPER else [])
    supers = SUPERS * G + len(tail)
    ROWS = G + 1
    assert ROWS <= P
    widths = [P] * SUPERS

    def view_nodes(t):
        return t.rearrange("(p j) d -> p (j d)", j=NJ)

    def started(value):
        return not isinstance(value, int) or value > 0

    with ExitStack() as ctx:
        def dram(name, shape, dt):
            return nc.dram_tensor(name, shape, dt).ap()

        def sb(name, shape, dt=F32):
            return ctx.enter_context(nc.sbuf_tensor(name, shape, dt))

        def sem(name):
            return ctx.enter_context(nc.semaphore(name))

        h_dram = dram("h_scratch", [NP + WIN, D], F32)
        h2_dram = dram("h2_scratch", [NP, D], F32)
        acc_dram = [dram(f"acc_scratch{t}", [NP + P, D], F32) for t in range(TILES)]
        deg_dram = dram("deg_scratch", [NP], F32)

        X = sb("X", [P, NJ * D])
        src_col = sb("src_col", [P, ROWS * 16])
        rel_col = sb("rel_col", [P, ROWS * 16])
        w_col = sb("w_col", [P, ROWS * 16])
        bases = sb("bases", [1, ROWS * SUPERS], I32)
        ident = sb("ident", [P, P])
        ident_b = sb("ident_b", [P, P], BF16)
        earlier = sb("earlier", [P, P])
        lane = sb("lane", [P, WIN])
        win_node = sb("win_node", [P, windows])
        win_first = sb("win_first", [P, windows])
        dump_col = sb("dump_col", [P, 1])
        ones = sb("ones", [P, P])
        eps_col = sb("eps_col", [P, 1])
        ln_eps = sb("ln_eps", [P, 1])
        W1_sb = sb("W1_sb", [P, H])
        W2_sb = sb("W2_sb", [P, 2, D])
        b1_bc = sb("b1_bc", [P, H])
        b2_bc = sb("b2_bc", [P, D])
        gamma_col = sb("gamma_col", [P, 2])
        beta_col = sb("beta_col", [P, 2])
        flag_f = sb("flag_f", [1, 1])
        flag_i = sb("flag_i", [1, 1], I32)
        spread = sb("spread", [P, 4])
        mv = sb("mv", [P, 2, CHUNK, 2])
        stats = sb("stats", [P, 2, CHUNK, 6])
        std = sb("std", [P, 2, CHUNK])
        rstd = sb("rstd", [P, 2, CHUNK])
        nmr = sb("nmr", [P, 2, CHUNK])
        mv2 = sb("mv2", [P, CHUNK, 2])
        stats2 = sb("stats2", [P, CHUNK, 6])
        std2 = sb("std2", [P, CHUNK])
        rstd2 = sb("rstd2", [P, CHUNK])
        nmr2 = sb("nmr2", [P, CHUNK])
        deg_nodes = sb("deg_nodes", [P, NJ])

        aggT_words = NP + WIN
        arena_words = max(2 * aggT_words, 23040)
        arena = sb("arena", [P, arena_words])
        parts_at = arena_words - 2 * GROUP
        src_hi, src_lo, rel_hi, rel_lo = (
            arena[:, parts_at + n * GROUP // 2:parts_at + (n + 1) * GROUP // 2].bitcast(BF16) for n in range(4))
        place = [0]

        def area(words, restart=False):
            if restart:
                place[0] = 0
            a = arena[:, place[0]:place[0] + words]
            place[0] += words
            assert place[0] <= arena_words
            return a

        dst_i = area(GROUP, True).bitcast(I32)
        src_i = area(GROUP).bitcast(I32)
        w_rows = area(GROUP)
        dst_f = area(GROUP)
        src_f = area(GROUP)
        rel_f = area(GROUP)
        part_i = area(GROUP).bitcast(I32)
        h_out = area(2 * CHUNK * D).rearrange("p (b n) -> p b n", b=2)
        eh_out = area(2 * CHUNK * D).rearrange("p (b n) -> p b n", b=2)
        zeros = area(CHUNK * D)
        ea = area(SUPERS * TILES * D, True).rearrange("p (c t d) -> p c t d", c=SUPERS, t=TILES)
        hwin = area(SUPERS * D).rearrange("p (c d) -> p c d", c=SUPERS)
        onehotT = area(2 * SUPER).rearrange("p (b e) -> p b e", b=2)
        same = area(2 * TILES * P).rearrange("p (b t e) -> p b t e", b=2, t=TILES)
        masked = area(2 * TILES * P).rearrange("p (b t e) -> p b t e", b=2, t=TILES)
        summed = area(2 * TILES * D).rearrange("p (b t d) -> p b t d", b=2, t=TILES)
        before = area(2 * TILES).rearrange("p (b t) -> p b t", b=2)
        dump_or_0 = area(2 * TILES).rearrange("p (b t) -> p b t", b=2)
        scatter_idx = area(SUPERS * TILES).bitcast(I32).rearrange("p (c t) -> p c t", c=SUPERS)
        accs = area(2 * TILES * CHUNK * D, True).rearrange("p (b r n) -> p b r n", b=2, r=TILES)
        nodesT = area(2 * D).rearrange("p (b d) -> p b d", b=2)
        h1 = area(2 * CHUNK * H).rearrange("p (b j f) -> p b j f", b=2, j=CHUNK)
        reluT = area(2 * 2 * P).rearrange("p (b s n) -> p b s n", b=2, s=2)
        h2_out = area(2 * CHUNK * D).rearrange("p (b n) -> p b n", b=2)
        aggT = area(aggT_words, True)
        deg = area(aggT_words)[0:1, :]
        gathered = sb("gathered", [P, SUPERS, TILES, D])
        gather_idx = sb("gather_idx", [P, SUPERS, TILES], I32)
        rel_win = sb("rel_win", [P, 2, TILES])
        onehot = sb("onehot", [P, 2, TILES, WIN])
        aggT_chunk = arena[:, aggT_words:aggT_words + 2 * CHUNK * P].rearrange(
            "p (b j n) -> p b j n", b=2, j=CHUNK)
        h2_in = arena[:, aggT_words + 2 * CHUNK * P:aggT_words + 2 * CHUNK * (P + D)].rearrange(
            "p (b j d) -> p b j d", b=2, j=CHUNK)
        no_edge = sb("no_edge", [P, NJ])
        base_col = sb("base_col", [P, SUPERS])

        bank = [ctx.enter_context(nc.psum_tensor(f"bank{b}", [P, 512], F32)) for b in range(8)]
        dst_bc, src_bc, gath_ps, sum_ps = bank[0:2], bank[2:4], bank[4:6], bank[6:8]
        nodesT_ps, h1_ps, hnT_ps, mlp_ps = bank[0:2], bank[2:4], bank[4:6], bank[6:8]
        agg_ps, deg_ps = bank[0:2], bank[2:4]

        idx_loaded = sem("idx_loaded")
        idx_zeroed = sem("idx_zeroed")
        const_ready = sem("const_ready")
        weights_loaded = sem("weights_loaded")
        x_zeroed = sem("x_zeroed")
        x_loaded = sem("x_loaded")
        prep = sem("prep")
        REL_MADE, WAY_OUT_MADE, FLAG_MADE, ROWS_MADE, PARTS_MADE = 2, 6, 8, 12, 19
        way_out_turned = sem("way_out_turned")
        flag_spread = sem("flag_spread")
        h_made = sem("h_made")
        eps1_ready = sem("eps1_ready")
        eh_ready = sem("eh_ready")
        sums_added = sem("sums_added")
        pool_turns = sem("pool_turns")
        dve_turns = sem("dve_turns")
        rel_cut = sem("rel_cut")
        flag_ready = sem("flag_ready")
        col_turned = sem("col_turned")
        col_ready = sem("col_ready")
        zeros_ready = sem("zeros_ready")
        cleared = sem("cleared")
        ln_stats = sem("ln_stats")
        ln_mv = sem("ln_mv")
        ln_std = sem("ln_std")
        ln_rstd = sem("ln_rstd")
        ln_nmr = sem("ln_nmr")
        h_stored = [sem(f"h_stored{b}") for b in range(2)]
        eh_stored = [sem(f"eh_stored{b}") for b in range(2)]
        ea_landed = [sem(f"ea_landed{c}") for c in range(SUPERS)]
        hwin_landed = [sem(f"hwin_landed{c}") for c in range(SUPERS)]
        dst_spread = sem("dst_spread")
        src_spread = sem("src_spread")
        onehotT_ready = sem("onehotT_ready")
        h_gathered = sem("h_gathered")
        h_added = sem("h_added")
        message_ready = sem("message_ready")
        same_ready = sem("same_ready")
        before_ready = sem("before_ready")
        dump_ready = sem("dump_ready")
        scatter_idx_ready = sem("scatter_idx_ready")
        merged = sem("merged")
        summed_ready = sem("summed_ready")
        scattered = [sem(f"scattered{t}") for t in range(TILES)]
        accs_landed = [sem(f"accs_landed{b}") for b in range(2)]
        pool_summed = sem("pool_summed")
        half_summed = sem("half_summed")
        nodes_ready = sem("nodes_ready")
        nodes_turned = sem("nodes_turned")
        nodesT_ready = sem("nodesT_ready")
        h1_done = sem("h1_done")
        h1_ready = sem("h1_ready")
        mlp_stats = sem("mlp_stats")
        mlp_mv = sem("mlp_mv")
        mlp_std = sem("mlp_std")
        mlp_rstd = sem("mlp_rstd")
        mlp_nmr = sem("mlp_nmr")
        hn_ready = sem("hn_ready")
        hn_turned = sem("hn_turned")
        reluT_ready = sem("reluT_ready")
        mlp_done = sem("mlp_done")
        b2_added = sem("b2_added")
        x1_ready = sem("x1_ready")
        ln2_stats = sem("ln2_stats")
        ln2_mv = sem("ln2_mv")
        ln2_std = sem("ln2_std")
        ln2_rstd = sem("ln2_rstd")
        ln2_nmr = sem("ln2_nmr")
        h2_ready = sem("h2_ready")
        h2_stored = [sem(f"h2_stored{b}") for b in range(2)]
        agg_zeroed = sem("agg_zeroed")
        deg_zeroed = sem("deg_zeroed")
        gather_idx_ready = sem("gather_idx_ready")
        gathered_landed = [sem(f"gathered_landed{c}") for c in range(SUPERS)]
        weighted = sem("weighted")
        rel_shifted = sem("rel_shifted")
        onehot_ready = sem("onehot_ready")
        agg_done = sem("agg_done")
        agg_added = sem("agg_added")
        deg_stored = sem("deg_stored")
        deg_loaded = sem("deg_loaded")
        no_edge_ready = sem("no_edge_ready")
        h2_loaded = [sem(f"h2_loaded{b}") for b in range(2)]
        agg_copied = sem("agg_copied")
        agg_turned = sem("agg_turned")
        own_added = sem("own_added")
        result_ready = sem("result_ready")
        stored = sem("stored")

        CONSTS = 11
        WEIGHTS = 7

        def part_cuts(n):
            cut = n // 16 * 16
            return [(a, b) for a, b in ((0, cut), (cut, n)) if b > a]

        node_cuts = [(a, b, NJ) for a, b in part_cuts(full_parts)]
        if rest_nodes:
            node_cuts.append((full_parts, full_parts + 1, rest_nodes))
        row_cuts = [(a, b, GROUP) for a, b in part_cuts(G)] + [(G, G + 1, rest)]

        def both_ways(eng, program):
            fast = eng.value_load(flag_i[0:1, 0:1], min_val=0, max_val=1)
            with eng.If(fast):
                program(1)
            with eng.Else():
                program(windows)

        def over_groups(eng, group):
            group(0, widths)
            with eng.Fori(1, G) as k:
                group(k, widths)
            group(G, tail)

        def over_chunks(eng, pair):
            pair(0)
            if chunks > 2:
                with eng.Fori(1, chunks // 2) as m:
                    pair(m)

        def over_windows(eng, nw, step):
            if nw == 1:
                step(0)
            else:
                with eng.Fori(0, nw) as w:
                    step(w)

        def cols(i):
            return bass.ds(TILES * i, TILES)

        block = ctx.enter_context(nc.Block())

        @block.sync
        def _(sp):
            sp.wait_ge(idx_zeroed, 3)
            for rows, of in ((dst_i, dst), (src_i, src), (w_rows, edge_weight)):
                for a, b, n in row_cuts:
                    sp.dma_start(rows[a:b, 0:n], of[a * GROUP:a * GROUP + (b - a) * n].rearrange(
                        "(k e) -> k e", e=n)).then_inc(idx_loaded, 16)
            with nc.allow_non_contiguous_dma(reason="one dst of each supertile, once"):
                nb = -(-E // SUPER)
                sp.dma_start(bases[0:1, 0:nb - 1], dst[0:(nb - 1) * SUPER].rearrange(
                    "(a s e) -> a s e", a=1, e=SUPER)[:, :, 0]).then_inc(idx_loaded, 16)
                sp.dma_start(bases[0:1, nb - 1:nb], dst[(nb - 1) * SUPER:(nb - 1) * SUPER + 1].rearrange(
                    "(a s) -> a s", a=1)).then_inc(idx_loaded, 16)
                sp.dma_start(gamma_col[:, :], gamma.rearrange("(s p) -> p s", p=P)).then_inc(weights_loaded, 16)
                sp.dma_start(beta_col[:, :], beta.rearrange("(s p) -> p s", p=P)).then_inc(weights_loaded, 16)
            sp.wait_ge(x_zeroed, 1)
            for a, b, n in node_cuts:
                sp.dma_start(X[a:b, 0:n * D], x[a * NJ:a * NJ + (b - a) * n, :].rearrange(
                    "(p j) d -> p (j d)", j=n)).then_inc(x_loaded, 16)
            sp.dma_start(W1_sb[:, :], W1).then_inc(weights_loaded, 16)
            sp.dma_start(W2_sb[:, :, :], W2.rearrange("(s p) d -> p s d", p=P)).then_inc(weights_loaded, 16)
            for row, of in ((b1_bc, b1), (b2_bc, b2), (eps_col, eps)):
                sp.dma_start(row[:, :], of.rearrange("(a n) -> a n", a=1).to_broadcast(row.shape)).then_inc(
                    weights_loaded, 16)

            sp.wait_ge(zeros_ready, 1)
            for t in range(TILES):
                if t:
                    sp.dma_start(
                        acc_dram[t][0:NP, :].rearrange("(p q n) d -> p q (n d)", p=P, q=chunks),
                        zeros[:, :].rearrange("p (a n) -> p a n", a=1).to_broadcast([P, chunks, CHUNK * D]),
                    ).then_inc(cleared, 16)
                sp.dma_start(acc_dram[t][DUMP:DUMP + P, :], zeros[:, 0:D]).then_inc(cleared, 16)
            sp.dma_start(h_dram[NP:NP + WIN, :], zeros[0:WIN, 0:D]).then_inc(cleared, 16)

            def store_h(m):
                for b in range(2):
                    q = 2 * m + b
                    sp.wait_ge(h_made, q + 1)
                    sp.wait_ge(eh_ready, q + 1)
                    at = bass.ds(q * CHUNK * D, CHUNK * D)
                    sp.dma_start(view_nodes(h_dram[0:NP, :])[:, at], h_out[:, b, :]).then_inc(h_stored[b], 16)
                    sp.dma_start(view_nodes(acc_dram[0][0:NP, :])[:, at], eh_out[:, b, :]).then_inc(
                        eh_stored[b], 16)

            over_chunks(sp, store_h)

            for b in range(2):
                sp.wait_ge(h_stored[b], 16 * (chunks // 2))
                sp.wait_ge(eh_stored[b], 16 * (chunks // 2))
            sp.wait_ge(cleared, 16 * 2 * TILES)
            sp.wait_ge(flag_ready, 1)
            sp.wait_ge(prep, PARTS_MADE)
            sp.wait_ge(col_ready, 3 * SUPERS)

            def loads(nw):
                def group(k, parts):
                    for c, n in enumerate(parts):
                        i = SUPERS * k + c
                        if started(k):
                            sp.wait_ge(merged, i - SUPERS + 1)
                        sp.dma_start(ea[0:n, c, :, :], edge_attr[bass.ds(SUPER * i, n * TILES), :].rearrange(
                            "(p t) d -> p t d", t=TILES)).then_inc(ea_landed[c], 16)

                        def window(w):
                            step = i * nw + w
                            last = i - SUPERS + 1 if nw == 1 else step
                            if started(last):
                                sp.wait_ge(h_gathered, last)
                            if nw == 1:
                                base = sp.value_load(bases[0:1, bass.ds(i, 1)], min_val=0, max_val=N - 1)
                            else:
                                base = w * WIN
                            sp.dma_start(hwin[0:WIN, c, :], h_dram[bass.ds(base, WIN), :]).then_inc(
                                hwin_landed[c], 16)

                        over_windows(sp, nw, window)

                over_groups(sp, group)

            both_ways(sp, loads)

            for t in range(TILES):
                sp.wait_ge(scattered[t], 16 * supers)

            def node_loads(m):
                for b in range(2):
                    q = 2 * m + b
                    if started(CHUNK * (q - 1)):
                        sp.wait_ge(nodes_turned, CHUNK * (q - 1))
                    for t in range(TILES):
                        sp.dma_start(accs[:, b, t, :], view_nodes(acc_dram[t][0:NP, :])[
                            :, bass.ds(q * CHUNK * D, CHUNK * D)]).then_inc(accs_landed[b], 16)

            over_chunks(sp, node_loads)

            sp.wait_ge(agg_added, 1)
            sp.dma_start(deg_dram.rearrange("(a n) -> a n", a=1), deg[:, 0:NP]).then_inc(deg_stored, 16)
            sp.wait_ge(deg_stored, 16)
            sp.dma_start(deg_nodes[:, :], deg_dram.rearrange("(p j) -> p j", j=NJ)).then_inc(deg_loaded, 16)

            def result_loads(m):
                for b in range(2):
                    q = 2 * m + b
                    if started(CHUNK * (q - 1)):
                        sp.wait_ge(own_added, CHUNK * (q - 1))
                    sp.dma_start(h2_in[:, b, :, :], h2_dram.rearrange("(p j) d -> p j d", j=NJ)[
                        :, bass.ds(q * CHUNK, CHUNK), :]).then_inc(h2_loaded[b], 16)

            over_chunks(sp, result_loads)

            sp.wait_ge(result_ready, 2 * chunks)
            for a, b, n in node_cuts:
                sp.dma_start(out[a * NJ:a * NJ + (b - a) * n, :].rearrange("(p j) d -> p (j d)", j=n),
                             X[a:b, 0:n * D]).then_inc(stored, 16)
            sp.wait_ge(stored, 16 * len(node_cuts))

        @block.gpsimd
        def _(pool):
            for rows in (dst_i, src_i, w_rows):
                nc.gpsimd.memset(rows, 0).then_inc(idx_zeroed, 1)
            nc.gpsimd.memset(zeros, 0.0).then_inc(zeros_ready, 1)
            nc.gpsimd.memset(ident[:, :], 0.0).then_inc(const_ready, 1)
            nc.gpsimd.memset(earlier[:, :], 1.0).then_inc(const_ready, 1)
            nc.gpsimd.memset(ones[:, :], 1.0).then_inc(const_ready, 1)
            nc.gpsimd.memset(ln_eps[:, :], LN_EPS).then_inc(const_ready, 1)
            nc.gpsimd.iota(lane[:, :], pattern=[[1, WIN]], base=0, channel_multiplier=0,
                           allow_small_or_imprecise_dtypes=True).then_inc(const_ready, 1)
            nc.gpsimd.iota(win_node[:, :], pattern=[[WIN, windows]], base=0, channel_multiplier=1,
                           allow_small_or_imprecise_dtypes=True).then_inc(const_ready, 1)
            nc.gpsimd.iota(win_first[:, :], pattern=[[WIN, windows]], base=0, channel_multiplier=0,
                           allow_small_or_imprecise_dtypes=True).then_inc(const_ready, 1)
            nc.gpsimd.iota(dump_col[:, :], pattern=[[0, 1]], base=DUMP, channel_multiplier=1,
                           allow_small_or_imprecise_dtypes=True).then_inc(const_ready, 1)
            pool.wait_ge(const_ready, 8)
            nc.gpsimd.affine_select(out=ident[:, :], in_=ident[:, :], compare_op=ALU.not_equal, fill=1.0,
                                    base=0, pattern=[[-1, P]], channel_multiplier=1).then_inc(const_ready, 1)
            nc.gpsimd.affine_select(out=earlier[:, :], in_=earlier[:, :], compare_op=ALU.is_ge, fill=0.0,
                                    base=-1, pattern=[[-1, P]], channel_multiplier=1).then_inc(const_ready, 1)
            pool.wait_ge(const_ready, 10)
            nc.gpsimd.tensor_copy(ident_b[:, :], ident[:, :]).then_inc(const_ready, 1)
            pool.wait_ge(prep, REL_MADE)
            nc.gpsimd.affine_select(out=rel_f, in_=rel_f, compare_op=ALU.is_ge, fill=0.0, base=E - 1,
                                    pattern=[[-1, GROUP]], channel_multiplier=-GROUP).then_inc(rel_cut, 1)

            pool.wait_ge(eps1_ready, 1)

            def scale_h(m):
                for b in range(2):
                    q = 2 * m + b
                    pool.wait_ge(h_made, q + 1)
                    if started(m):
                        pool.wait_ge(eh_stored[b], 16 * m)
                    pool.sem_inc(pool_turns, 1)
                    nc.gpsimd.tensor_scalar(eh_out[:, b, :], h_out[:, b, :], eps_col[:, 0:1], None,
                                            ALU.mult).then_inc(eh_ready, 1)

            over_chunks(pool, scale_h)

            pool.wait_ge(cleared, 16 * 2 * TILES)
            for b in range(2):
                pool.wait_ge(eh_stored[b], 16 * (chunks // 2))

            def scatter(k, parts):
                for c, n in enumerate(parts):
                    i = SUPERS * k + c
                    pool.wait_ge(scatter_idx_ready, i + 1)
                    pool.wait_ge(summed_ready, i + 1)
                    for t in range(TILES):
                        if started(i):
                            pool.wait_ge(scattered[t], 16 * i)
                        pool.sem_inc(pool_turns, 1)
                        nc.gpsimd.indirect_dma_start(
                            acc_dram[t], bass.IndirectOffsetOnAxis(scatter_idx[0:n, c, t:t + 1], 0),
                            summed[0:n, c % 2, t, :], None, compute_op=ALU.add).then_inc(scattered[t], 16)

            over_groups(pool, scatter)

            def sum_half(b, m):
                pool.wait_ge(accs_landed[b], 16 * TILES * (m + 1))
                nc.gpsimd.tensor_tensor(accs[:, b, 2, :], accs[:, b, 2, :], accs[:, b, 3, :], ALU.add).then_inc(
                    pool_summed, 1)

            def norm(b, q):
                pool.wait_ge(mlp_nmr, q + 1)
                pool.sem_inc(pool_turns, 1)
                for j in range(CHUNK):
                    nc.gpsimd.tensor_scalar(h1[:, b, j, :], h1[:, b, j, :], rstd[:, b, j:j + 1],
                                            nmr[:, b, j:j + 1], ALU.mult, ALU.add).then_inc(hn_ready, 1)

            def pair(m):
                sum_half(0, m)
                if started(m):
                    norm(1, 2 * m - 1)
                sum_half(1, m)
                norm(0, 2 * m)

            over_chunks(pool, pair)
            norm(1, chunks - 1)

            for b in range(2):
                pool.wait_ge(h2_stored[b], 16 * (chunks // 2))

            def gathers(nw):
                def group(k, parts):
                    for c, n in enumerate(parts):
                        i = SUPERS * k + c
                        pool.wait_ge(gather_idx_ready, i + 1)
                        if started(i - SUPERS + 1):
                            pool.wait_ge(agg_done, (i - SUPERS + 1) * nw)
                        pool.sem_inc(pool_turns, 1)
                        for t in range(TILES):
                            nc.gpsimd.indirect_dma_start(
                                gathered[0:n, c, t, :], None, h2_dram,
                                bass.IndirectOffsetOnAxis(gather_idx[0:n, c, t:t + 1], 0)).then_inc(gathered_landed[c], 16)

                over_groups(pool, group)

            both_ways(pool, gathers)

            pool.wait_ge(deg_stored, 16)
            sums = aggT[:, 0:NP].rearrange("f (p j) -> f j p", j=NJ)

            def copies(m):
                for b in range(2):
                    q = 2 * m + b
                    if started(q - 1):
                        pool.wait_ge(agg_turned, q - 1)
                    nc.gpsimd.tensor_copy(aggT_chunk[:, b, :, :], sums[:, bass.ds(q * CHUNK, CHUNK), :]).then_inc(
                        agg_copied, 1)

            over_chunks(pool, copies)

        @block.tensor
        def _(pe):
            pe.wait_ge(const_ready, CONSTS)
            pe.wait_ge(prep, WAY_OUT_MADE)
            nc.tensor.transpose(bank[0][0:1, 0:P], spread[:, 3:4], ident[:, :]).then_inc(way_out_turned, 1)
            pe.wait_ge(prep, FLAG_MADE)
            nc.tensor.matmul(bank[1][:, 0:1], ones[0:1, :], flag_f[:, :], start=True, stop=True).then_inc(
                flag_spread, 1)
            pe.wait_ge(prep, ROWS_MADE)
            n = 0
            for rows in (src_f, rel_f, w_rows):
                for c in range(SUPERS):
                    if n >= 2:
                        pe.wait_ge(col_ready, n - 1)
                    for t in range(TILES):
                        last = nc.tensor.transpose(bank[2 + n % 2][:, t * P:(t + 1) * P],
                                                   rows[:, c * SUPER + t:(c + 1) * SUPER:TILES], ident[:, :])
                    last.then_inc(col_turned, 1)
                    n += 1

            pe.wait_ge(flag_ready, 1)
            pe.wait_ge(prep, PARTS_MADE)
            pe.wait_ge(col_ready, 3 * SUPERS)

            def edges(nw):
                def spread_rows(k, c, i):
                    b = c % 2
                    pick = ident_b[:, bass.ds(k, 1)].to_broadcast([P, P])
                    e = slice(c * SUPER, (c + 1) * SUPER)
                    if started((i - 1) * nw):
                        pe.wait_ge(onehotT_ready, (i - 1) * nw)
                    nc.tensor.matmul(dst_bc[b][:, :], pick, rel_hi[:, e], start=True, stop=False)
                    nc.tensor.matmul(dst_bc[b][:, :], pick, rel_lo[:, e], start=False, stop=True).then_inc(
                        dst_spread, 1)
                    if started(i - 1):
                        pe.wait_ge(same_ready, i - 1)
                    nc.tensor.matmul(src_bc[b][:, :], pick, src_hi[:, e], start=True, stop=False)
                    nc.tensor.matmul(src_bc[b][:, :], pick, src_lo[:, e], start=False, stop=True).then_inc(
                        src_spread, 1)

                def gather(k, c, n, i):
                    b = c % 2

                    def window(w):
                        step = i * nw + w
                        pe.wait_ge(onehotT_ready, step + 1)
                        pe.wait_ge(hwin_landed[c], 16 * (k * nw + w + 1))
                        last = i - 1 if nw == 1 else step
                        if started(last):
                            pe.wait_ge(h_added, last)
                        for t in range(TILES):
                            mm = nc.tensor.matmul(gath_ps[b][0:n, t * D:(t + 1) * D],
                                                  onehotT[0:WIN, b, t:n * TILES:TILES], hwin[0:WIN, c, :],
                                                  start=True, stop=True)
                        mm.then_inc(h_gathered, 1)

                    over_windows(pe, nw, window)

                def merge(c, n, i):
                    b = c % 2
                    pe.wait_ge(same_ready, i + 1)
                    pe.wait_ge(message_ready, i + 1)
                    if started(i - 1):
                        pe.wait_ge(summed_ready, i - 1)
                    for t in range(TILES):
                        mm = nc.tensor.matmul(sum_ps[b][0:n, t * D:(t + 1) * D], same[0:n, b, t, 0:n],
                                              ea[0:n, c, t, :], start=True, stop=True)
                    mm.then_inc(merged, 1)

                def group(k, parts, following):
                    for c, n in enumerate(parts):
                        i = SUPERS * k + c
                        ahead = (k, c + 1, parts[c + 1]) if c + 1 < len(parts) else following
                        if ahead:
                            spread_rows(ahead[0], ahead[1], i + 1)
                        merge(c, n, i)
                        if ahead:
                            gather(*ahead, i + 1)

                spread_rows(0, 0, 0)
                gather(0, 0, P, 0)
                group(0, widths, (1, 0, P))
                with pe.Fori(1, G) as k:
                    group(k, widths, (k + 1, 0, P))
                group(G, tail, None)

            both_ways(pe, edges)

            for t in range(TILES):
                pe.wait_ge(scattered[t], 16 * supers)
            pe.wait_ge(weights_loaded, 16 * WEIGHTS)

            def first_product(b, q):
                pe.wait_ge(nodes_ready, q + 1)
                for j in range(CHUNK):
                    n = CHUNK * q + j
                    s = (CHUNK * b + j) % 2
                    if started(n - 1):
                        pe.wait_ge(nodesT_ready, n - 1)
                    nc.tensor.transpose(nodesT_ps[s][:, 0:P], accs[:, b, 0, j * D:(j + 1) * D],
                                        ident[:, :]).then_inc(nodes_turned, 1)
                    pe.wait_ge(nodesT_ready, n + 1)
                    if started(n - 1):
                        pe.wait_ge(h1_ready, n - 1)
                    nc.tensor.matmul(h1_ps[s][:, 0:H], nodesT[:, s, :], W1_sb[:, :], start=True,
                                     stop=True).then_inc(h1_done, 1)

            def second_product(b, q):
                for j in range(CHUNK):
                    n = CHUNK * q + j
                    s = (CHUNK * b + j) % 2
                    pe.wait_ge(hn_ready, n + 1)
                    if started(n - 1):
                        pe.wait_ge(reluT_ready, 2 * (n - 1))
                    for half in range(2):
                        turn = nc.tensor.transpose(hnT_ps[s][:, half * P:(half + 1) * P],
                                                   h1[:, b, j, half * P:(half + 1) * P], ident[:, :])
                    turn.then_inc(hn_turned, 1)
                    pe.wait_ge(reluT_ready, 2 * (n + 1))
                    if started(n - 1):
                        pe.wait_ge(x1_ready, n - 1)
                    for half in range(2):
                        mm = nc.tensor.matmul(mlp_ps[s][:, 0:D], reluT[:, s, half, :], W2_sb[:, half, :],
                                              start=half == 0, stop=half == 1)
                    mm.then_inc(mlp_done, 1)

            def pair(m):
                first_product(0, 2 * m)
                if started(m):
                    second_product(1, 2 * m - 1)
                first_product(1, 2 * m + 1)
                second_product(0, 2 * m)

            over_chunks(pe, pair)
            second_product(1, chunks - 1)

            def sums(nw):
                def group(k, parts):
                    for c, n in enumerate(parts):
                        i = SUPERS * k + c
                        b = c % 2

                        def window(w):
                            step = i * nw + w
                            pe.wait_ge(weighted, i + 1)
                            pe.wait_ge(onehot_ready, step + 1)
                            for t in range(TILES):
                                nc.tensor.matmul(agg_ps[b][:, 0:WIN], gathered[0:n, c, t, :], onehot[0:n, b, t, :],
                                                 start=t == 0, stop=t == TILES - 1)
                            for t in range(TILES):
                                mm = nc.tensor.matmul(deg_ps[b][0:1, 0:WIN], ones[0:n, 0:1], onehot[0:n, b, t, :],
                                                      start=t == 0, stop=t == TILES - 1)
                            mm.then_inc(agg_done, 1)

                        over_windows(pe, nw, window)

                over_groups(pe, group)

            both_ways(pe, sums)

            pe.wait_ge(agg_added, 1)

            def turns(m):
                for b in range(2):
                    q = 2 * m + b
                    pe.wait_ge(agg_copied, q + 1)
                    if started(q - 1):
                        pe.wait_ge(result_ready, 2 * (q - 1))
                    for j in range(CHUNK):
                        turn = nc.tensor.transpose(bank[4 + 2 * b + j // 4][:, j % 4 * D:j % 4 * D + D],
                                                   aggT_chunk[:, b, j, :], ident[:, :])
                    turn.then_inc(agg_turned, 1)

            over_chunks(pe, turns)

        @block.scalar
        def _(act):
            n = 0
            for col in (src_col, rel_col, w_col):
                for c in range(SUPERS):
                    act.wait_ge(col_turned, n + 1)
                    nc.scalar.copy(
                        col[:, :].rearrange("p (k c t) -> p c t k", c=SUPERS, t=TILES)[:, c, :, :],
                        bank[2 + n % 2][:, :].rearrange("p (t k) -> p t k", t=TILES)[:, :, 0:ROWS],
                    ).then_inc(col_ready, 1)
                    n += 1

            act.wait_ge(const_ready, CONSTS)
            act.wait_ge(weights_loaded, 16 * WEIGHTS)

            def norm_x(m):
                for b in range(2):
                    q = 2 * m + b
                    act.wait_ge(ln_mv, CHUNK * (q + 1))
                    nc.scalar.activation(std[:, b, :], mv[:, b, :, 1], ACT.Sqrt, bias=ln_eps[:, 0:1]).then_inc(
                        ln_std, 1)
                    act.wait_ge(ln_nmr, q + 1)
                    if started(m):
                        act.wait_ge(h_stored[b], 16 * m)
                        act.wait_ge(eh_stored[b], 16 * m)
                    for j in range(CHUNK):
                        last = nc.scalar.activation(h_out[:, b, j * D:(j + 1) * D],
                                                    X[:, bass.ds((q * CHUNK + j) * D, D)], ACT.Relu,
                                                    scale=rstd[:, b, j:j + 1], bias=nmr[:, b, j:j + 1])
                    last.then_inc(h_made, 1)

            over_chunks(act, norm_x)

            act.wait_ge(flag_ready, 1)
            for b in range(2):
                act.wait_ge(h_stored[b], 16 * (chunks // 2))

            def messages(nw):
                def group(k, parts):
                    for c, n in enumerate(parts):
                        i = SUPERS * k + c
                        b = c % 2
                        act.wait_ge(h_added, (i + 1) * nw)
                        nc.scalar.activation(ea[0:n, c, :, :], ea[0:n, c, :, :], ACT.Relu).then_inc(message_ready, 1)
                        act.wait_ge(merged, i + 1)
                        if started(i - 1):
                            for t in range(TILES):
                                act.wait_ge(scattered[t], 16 * (i - 1))
                        nc.scalar.copy(summed[0:n, b, :, :], sum_ps[b][0:n, :].rearrange(
                            "p (t d) -> p t d", t=TILES)).then_inc(summed_ready, 1)

                over_groups(act, group)

            both_ways(act, messages)

            for t in range(TILES):
                act.wait_ge(scattered[t], 16 * supers)

            def first_product(b, q):
                for j in range(CHUNK):
                    n = CHUNK * q + j
                    s = (CHUNK * b + j) % 2
                    act.wait_ge(nodes_turned, n + 1)
                    if started(n - 1):
                        act.wait_ge(h1_done, n - 1)
                    nc.scalar.copy(nodesT[:, s, :], nodesT_ps[s][:, 0:P]).then_inc(nodesT_ready, 1)
                act.wait_ge(mlp_mv, CHUNK * (q + 1))
                nc.scalar.activation(std[:, b, :], mv[:, b, :, 1], ACT.Sqrt, bias=ln_eps[:, 0:1]).then_inc(mlp_std, 1)

            def second_product(b, q, m):
                for j in range(CHUNK):
                    n = CHUNK * q + j
                    s = (CHUNK * b + j) % 2
                    act.wait_ge(hn_turned, n + 1)
                    if started(n - 1):
                        act.wait_ge(mlp_done, n - 1)
                    for half in range(2):
                        nc.scalar.activation(reluT[:, s, half, :], hnT_ps[s][:, half * P:(half + 1) * P], ACT.Relu,
                                             scale=gamma_col[:, half:half + 1],
                                             bias=beta_col[:, half:half + 1]).then_inc(reluT_ready, 1)
                act.wait_ge(ln2_mv, CHUNK * (q + 1))
                nc.scalar.activation(std2[:, :], mv2[:, :, 1], ACT.Sqrt, bias=ln_eps[:, 0:1]).then_inc(ln2_std, 1)
                act.wait_ge(ln2_nmr, q + 1)
                if started(m):
                    act.wait_ge(h2_stored[b], 16 * m)
                for j in range(CHUNK):
                    last = nc.scalar.activation(h2_out[:, b, j * D:(j + 1) * D],
                                                X[:, bass.ds((q * CHUNK + j) * D, D)], ACT.Relu,
                                                scale=rstd2[:, j:j + 1], bias=nmr2[:, j:j + 1])
                last.then_inc(h2_ready, 1)
                act.wait_ge(h2_ready, q + 1)
                act.dma_start(view_nodes(h2_dram)[:, bass.ds(q * CHUNK * D, CHUNK * D)], h2_out[:, b, :]).then_inc(
                    h2_stored[b], 16)

            def pair(m):
                first_product(0, 2 * m)
                if started(m):
                    second_product(1, 2 * m - 1, m - 1)
                first_product(1, 2 * m + 1)
                second_product(0, 2 * m, m)

            over_chunks(act, pair)
            second_product(1, chunks - 1, chunks // 2 - 1)

            for b in range(2):
                act.wait_ge(h2_stored[b], 16 * (chunks // 2))

            def indices(k, parts):
                for c, n in enumerate(parts):
                    i = SUPERS * k + c
                    if started(k):
                        act.wait_ge(gathered_landed[c], 16 * TILES * k)
                    nc.scalar.copy(gather_idx[0:n, c, :], src_col[0:n, cols(i)]).then_inc(gather_idx_ready, 1)

            indices(0, widths)
            nc.scalar.copy(deg, win_first[0:1, 0:1].to_broadcast([1, aggT_words])).then_inc(deg_zeroed, 1)
            with act.Fori(1, G) as k:
                indices(k, widths)
            indices(G, tail)

        @block.vector
        def _(dve):
            done = [0]

            def prep_step(ins):
                ins.then_inc(prep, 1)
                done[0] += 1
                dve.wait_ge(prep, done[0])

            def by_super(rows):
                return rows.rearrange("p (c e) -> p c e", c=SUPERS)

            nc.vector.memset(X[96:P, :], 0.0).then_inc(x_zeroed, 1)

            dve.wait_ge(idx_loaded, 16 * (3 * len(row_cuts) + 2))
            dve.wait_ge(const_ready, CONSTS)
            prep_step(nc.vector.tensor_copy(dst_f, dst_i))
            first = by_super(dst_f)[:, :, 0:1]
            prep_step(nc.vector.tensor_tensor(by_super(rel_f), by_super(dst_f),
                                              first.to_broadcast([P, SUPERS, SUPER]), ALU.subtract))
            dve.wait_ge(rel_cut, 1)
            prep_step(nc.vector.tensor_reduce(spread[:, 0:1], rel_f, AX_X, ALU.max))
            prep_step(nc.vector.tensor_reduce(spread[:, 1:2], rel_f, AX_X, ALU.min))
            prep_step(nc.vector.tensor_scalar(spread[:, 2:3], spread[:, 0:1], float(1 - WIN), None, ALU.add))
            prep_step(nc.vector.scalar_tensor_tensor(out=spread[:, 3:4], in0=spread[:, 1:2], scalar=-1.0,
                                                     in1=spread[:, 2:3], op0=ALU.mult, op1=ALU.max))
            assert done[0] == WAY_OUT_MADE
            dve.wait_ge(way_out_turned, 1)
            prep_step(nc.vector.tensor_reduce(spread[0:1, 0:1], bank[0][0:1, 0:P], AX_X, ALU.max))
            prep_step(nc.vector.tensor_scalar(flag_f[:, :], spread[0:1, 0:1], 0.0, None, ALU.is_le))
            assert done[0] == FLAG_MADE
            nc.vector.tensor_copy(flag_i[:, :], flag_f[:, :]).then_inc(flag_ready, 1)
            dve.wait_ge(flag_spread, 1)
            prep_step(nc.vector.tensor_copy(spread[:, 2:3], bank[1][:, 0:1]))
            prep_step(nc.vector.tensor_scalar(base_col[:, :], first.rearrange("p c a -> p (c a)"), spread[:, 2:3],
                                              None, ALU.mult))
            prep_step(nc.vector.tensor_tensor(
                by_super(rel_f), by_super(dst_f),
                base_col[:, :].rearrange("p (c a) -> p c a", a=1).to_broadcast([P, SUPERS, SUPER]), ALU.subtract))
            prep_step(nc.vector.tensor_copy(src_f, src_i))
            assert done[0] == ROWS_MADE
            prep_step(nc.vector.tensor_single_scalar(part_i, src_i, WIN - 1, op=ALU.bitwise_and))
            prep_step(nc.vector.tensor_tensor(src_hi, src_f, part_i, ALU.subtract))
            prep_step(nc.vector.tensor_copy(src_lo, part_i))
            prep_step(nc.vector.tensor_copy(dst_i, rel_f))
            prep_step(nc.vector.tensor_single_scalar(part_i, dst_i, WIN - 1, op=ALU.bitwise_and))
            prep_step(nc.vector.tensor_tensor(rel_hi, rel_f, part_i, ALU.subtract))
            prep_step(nc.vector.tensor_copy(rel_lo, part_i))
            assert done[0] == PARTS_MADE

            dve.wait_ge(weights_loaded, 16 * WEIGHTS)
            nc.vector.tensor_scalar(eps_col[:, :], eps_col[:, :], 1.0, None, ALU.add).then_inc(eps1_ready, 1)
            dve.wait_ge(x_loaded, 16 * len(node_cuts))

            def norm_x(m):
                for b in range(2):
                    q = 2 * m + b
                    for j in range(CHUNK):
                        nc.vector.bn_stats(stats[:, b, j, :], X[:, bass.ds((q * CHUNK + j) * D, D)]).then_inc(
                            ln_stats, 1)
                    dve.wait_ge(ln_stats, CHUNK * (q + 1))
                    dve.sem_inc(dve_turns, 1)
                    for j in range(CHUNK):
                        nc.vector.bn_aggr(mv[:, b, j, :], stats[:, b, j, :]).then_inc(ln_mv, 1)
                    dve.wait_ge(ln_std, q + 1)
                    if started(m):
                        dve.wait_ge(h_made, q - 1)
                    nc.vector.reciprocal(rstd[:, b, :], std[:, b, :]).then_inc(ln_rstd, 1)
                    dve.wait_ge(ln_rstd, q + 1)
                    nc.vector.scalar_tensor_tensor(out=nmr[:, b, :], in0=mv[:, b, :, 0], scalar=-1.0,
                                                   in1=rstd[:, b, :], op0=ALU.mult, op1=ALU.mult).then_inc(ln_nmr, 1)

            over_chunks(dve, norm_x)

            dve.wait_ge(flag_ready, 1)
            dve.wait_ge(col_ready, 3 * SUPERS)

            def messages(nw):
                def one_hot(c, n, i, step, w):
                    nc.vector.tensor_scalar(onehotT[0:WIN, c % 2, 0:n * TILES], dst_bc[c % 2][0:WIN, 0:n * TILES],
                                            win_node[0:WIN, bass.ds(w, 1)], None, ALU.is_equal).then_inc(
                                                onehotT_ready, 1)

                def merge_plan(c, n, i):
                    b = c % 2
                    dve.wait_ge(src_spread, i + 1)
                    if started(i - 1):
                        dve.wait_ge(merged, i - 1)
                    nc.vector.tensor_tensor(
                        same[0:n, b, :, 0:n],
                        src_bc[b][0:n, 0:n * TILES].rearrange("p (e t) -> p t e", t=TILES),
                        src_col[0:n, cols(i)].rearrange("p (t a) -> p t a", a=1).to_broadcast([n, TILES, n]),
                        ALU.is_equal).then_inc(same_ready, 1)
                    dve.wait_ge(same_ready, i + 1)
                    for t in range(TILES):
                        nc.vector.tensor_tensor_reduce(
                            out=masked[0:n, b, t, 0:n], in0=same[0:n, b, t, 0:n], in1=earlier[0:n, 0:n], scale=1.0,
                            scalar=0.0, op0=ALU.mult, op1=ALU.add,
                            accum_out=before[0:n, b, t:t + 1]).then_inc(before_ready, 1)
                    dve.wait_ge(before_ready, TILES * (i + 1))
                    nc.vector.tensor_scalar(dump_or_0[0:n, b, :], before[0:n, b, :], 1.0, dump_col[0:n, 0:1],
                                            ALU.min, ALU.mult).then_inc(dump_ready, 1)
                    dve.wait_ge(dump_ready, i + 1)
                    if started(i - 1):
                        dve.wait_ge(summed_ready, i - 1)
                    nc.vector.tensor_tensor(scatter_idx[0:n, c, :], dump_or_0[0:n, b, :], src_col[0:n, cols(i)],
                                            ALU.max).then_inc(scatter_idx_ready, 1)

                def add_h(c, n, k, i, step):
                    dve.wait_ge(ea_landed[c], 16 * (k + 1))
                    dve.wait_ge(h_gathered, step + 1)
                    if nw > 1 and started(step):
                        dve.wait_ge(h_added, step)
                    nc.vector.tensor_tensor(ea[0:n, c, :, :], ea[0:n, c, :, :], gath_ps[c % 2][0:n, :].rearrange(
                        "p (t d) -> p t d", t=TILES), ALU.add).then_inc(h_added, 1)

                def group(k, parts):
                    for c, n in enumerate(parts):
                        i = SUPERS * k + c
                        dve.wait_ge(dst_spread, i + 1)
                        if nw == 1:
                            one_hot(c, n, i, i, 0)
                            merge_plan(c, n, i)
                            add_h(c, n, k, i, i)
                        else:
                            merge_plan(c, n, i)
                            with dve.Fori(0, nw) as w:
                                one_hot(c, n, i, i * nw + w, w)
                                add_h(c, n, k, i, i * nw + w)

                over_groups(dve, group)

            both_ways(dve, messages)

            for t in range(TILES):
                dve.wait_ge(scattered[t], 16 * supers)

            def first_product(b, q, m):
                dve.wait_ge(accs_landed[b], 16 * TILES * (m + 1))
                nc.vector.tensor_tensor(accs[:, b, 0, :], accs[:, b, 0, :], accs[:, b, 1, :], ALU.add).then_inc(
                    half_summed, 1)
                dve.wait_ge(half_summed, q + 1)
                dve.wait_ge(pool_summed, q + 1)
                nc.vector.tensor_tensor(accs[:, b, 0, :], accs[:, b, 0, :], accs[:, b, 2, :], ALU.add).then_inc(
                    nodes_ready, 1)
                if started(m):
                    dve.wait_ge(hn_turned, CHUNK * (q - 1))
                for j in range(CHUNK):
                    n = CHUNK * q + j
                    dve.wait_ge(h1_done, n + 1)
                    nc.vector.tensor_tensor(h1[:, b, j, :], h1_ps[(CHUNK * b + j) % 2][:, 0:H], b1_bc[:, :],
                                            ALU.add).then_inc(h1_ready, 1)
                    dve.wait_ge(h1_ready, n + 1)
                    nc.vector.bn_stats(stats[:, b, j, :], h1[:, b, j, :]).then_inc(mlp_stats, 1)
                dve.wait_ge(mlp_stats, CHUNK * (q + 1))
                dve.sem_inc(dve_turns, 1)
                for j in range(CHUNK):
                    nc.vector.bn_aggr(mv[:, b, j, :], stats[:, b, j, :]).then_inc(mlp_mv, 1)
                dve.wait_ge(mlp_std, q + 1)
                nc.vector.reciprocal(rstd[:, b, :], std[:, b, :]).then_inc(mlp_rstd, 1)
                dve.wait_ge(mlp_rstd, q + 1)
                nc.vector.scalar_tensor_tensor(out=nmr[:, b, :], in0=mv[:, b, :, 0], scalar=-1.0,
                                               in1=rstd[:, b, :], op0=ALU.mult, op1=ALU.mult).then_inc(mlp_nmr, 1)

            def second_product(b, q):
                at = bass.ds(q * CHUNK * D, CHUNK * D)
                nc.vector.tensor_tensor(
                    X[:, at].rearrange("p (j d) -> p j d", d=D), X[:, at].rearrange("p (j d) -> p j d", d=D),
                    b2_bc[:, :].rearrange("p (a d) -> p a d", a=1).to_broadcast([P, CHUNK, D]),
                    ALU.add).then_inc(b2_added, 1)
                dve.wait_ge(b2_added, q + 1)
                for j in range(CHUNK):
                    n = CHUNK * q + j
                    own = X[:, bass.ds(n * D, D)]
                    dve.wait_ge(mlp_done, n + 1)
                    nc.vector.tensor_tensor(own, own, mlp_ps[(CHUNK * b + j) % 2][:, 0:D], ALU.add).then_inc(
                        x1_ready, 1)
                dve.wait_ge(x1_ready, CHUNK * (q + 1))
                dve.sem_inc(dve_turns, 1)
                for j in range(CHUNK):
                    nc.vector.bn_stats(stats2[:, j, :], X[:, bass.ds((q * CHUNK + j) * D, D)]).then_inc(ln2_stats, 1)
                dve.wait_ge(ln2_stats, CHUNK * (q + 1))
                dve.sem_inc(dve_turns, 1)
                for j in range(CHUNK):
                    nc.vector.bn_aggr(mv2[:, j, :], stats2[:, j, :]).then_inc(ln2_mv, 1)
                dve.wait_ge(ln2_std, q + 1)
                if started(q):
                    dve.wait_ge(h2_ready, q)
                nc.vector.reciprocal(rstd2[:, :], std2[:, :]).then_inc(ln2_rstd, 1)
                dve.wait_ge(ln2_rstd, q + 1)
                nc.vector.scalar_tensor_tensor(out=nmr2[:, :], in0=mv2[:, :, 0], scalar=-1.0,
                                               in1=rstd2[:, :], op0=ALU.mult, op1=ALU.mult).then_inc(ln2_nmr, 1)

            def pair(m):
                first_product(0, 2 * m, m)
                if started(m):
                    second_product(1, 2 * m - 1)
                first_product(1, 2 * m + 1, m)
                second_product(0, 2 * m)

            over_chunks(dve, pair)
            second_product(1, chunks - 1)

            for b in range(2):
                dve.wait_ge(h2_stored[b], 16 * (chunks // 2))
            nc.vector.memset(aggT, 0.0).then_inc(agg_zeroed, 1)
            dve.wait_ge(agg_zeroed, 1)
            dve.wait_ge(deg_zeroed, 1)

            def sums(nw):
                def group(k, parts):
                    for c, n in enumerate(parts):
                        i = SUPERS * k + c
                        b = c % 2
                        dve.wait_ge(gathered_landed[c], 16 * TILES * (k + 1))
                        nc.vector.tensor_tensor(
                            gathered[0:n, c, :, :], gathered[0:n, c, :, :],
                            w_col[0:n, cols(i)].rearrange("p (t a) -> p t a", a=1).to_broadcast([n, TILES, D]),
                            ALU.mult).then_inc(weighted, 1)

                        def window(w):
                            step = i * nw + w
                            if nw == 1:
                                rel = rel_col[0:n, cols(i)]
                            else:
                                nc.vector.tensor_scalar(rel_win[0:n, b, :], rel_col[0:n, cols(i)],
                                                        win_first[0:n, bass.ds(w, 1)], None,
                                                        ALU.subtract).then_inc(rel_shifted, 1)
                                dve.wait_ge(rel_shifted, step + 1)
                                rel = rel_win[0:n, b, :]
                            nc.vector.tensor_tensor(
                                onehot[0:n, b, :, :],
                                lane[0:n, :].rearrange("p (a v) -> p a v", a=1).to_broadcast([n, TILES, WIN]),
                                rel.rearrange("p (t a) -> p t a", a=1).to_broadcast([n, TILES, WIN]),
                                ALU.is_equal).then_inc(onehot_ready, 1)
                            base = dve.value_load(bases[0:1, bass.ds(i, 1)], min_val=0, max_val=N - 1) \
                                if nw == 1 else w * WIN
                            dve.wait_ge(agg_done, step + 1)
                            if started(step):
                                dve.wait_ge(sums_added, 2 * step)
                            at = bass.ds(base, WIN)
                            nc.vector.tensor_tensor(aggT[:, at], aggT[:, at], agg_ps[b][:, 0:WIN],
                                                    ALU.add).then_inc(sums_added, 1)
                            nc.vector.tensor_tensor(deg[:, at], deg[:, at], deg_ps[b][0:1, 0:WIN],
                                                    ALU.add).then_inc(sums_added, 1)

                        over_windows(dve, nw, window)

                over_groups(dve, group)
                dve.wait_ge(sums_added, 2 * supers * nw)

            both_ways(dve, sums)
            dve.sem_inc(agg_added, 1)

            dve.wait_ge(deg_loaded, 16)
            nc.vector.tensor_scalar(no_edge[:, :], deg_nodes[:, :], 0.0, None, ALU.is_equal).then_inc(no_edge_ready, 1)
            dve.wait_ge(no_edge_ready, 1)

            def results(m):
                for b in range(2):
                    q = 2 * m + b
                    dve.wait_ge(h2_loaded[b], 16 * (m + 1))
                    for j in range(CHUNK):
                        own = X[:, bass.ds((q * CHUNK + j) * D, D)]
                        nc.vector.scalar_tensor_tensor(
                            out=own, in0=h2_in[:, b, j, :], scalar=no_edge[:, bass.ds(q * CHUNK + j, 1)], in1=own,
                            op0=ALU.mult, op1=ALU.add).then_inc(own_added, 1)
                    dve.wait_ge(agg_turned, q + 1)
                    for j0, j1 in ((0, 4), (4, CHUNK)):
                        dve.wait_ge(own_added, q * CHUNK + j1)
                        own = X[:, bass.ds((q * CHUNK + j0) * D, (j1 - j0) * D)]
                        nc.vector.tensor_tensor(own, own, bank[4 + 2 * b + j0 // 4][:, 0:(j1 - j0) * D],
                                                ALU.add).then_inc(result_ready, 1)

            over_chunks(dve, results)


_INS = ["x", "src", "dst", "edge_attr_128", "edge_weight", "L0_gnn_eps", "L0_gnn_W1", "L0_gnn_b1",
        "L0_gnn_gamma", "L0_gnn_beta", "L0_gnn_W2", "L0_gnn_b2"]


def kernel(**inputs):
    import numpy as _np
    import concourse.bacc as _bacc
    from concourse import mybir as _mybir
    from concourse.bass_utils import run_bass_kernel_spmd as _run

    nc = _bacc.Bacc("TRN2", target_bir_lowering=False, num_devices=1)
    arrays, args = {}, []
    for name in _INS:
        a = _np.ascontiguousarray(inputs[name])
        arrays[f"in_{name}"] = a
        args.append(nc.dram_tensor(f"in_{name}", a.shape, _mybir.dt.from_np(a.dtype), kind="ExternalInput").ap())
    shape = arrays["in_x"].shape
    args.append(nc.dram_tensor("out_0", shape, _mybir.dt.float32, kind="ExternalOutput").ap())
    build(nc, *args)
    r = _run(nc, [arrays], core_ids=[0])
    return r.results[0]["out_0"]
```

```python
from contextlib import ExitStack

import concourse.bass as bass
from concourse import mybir

P = 128
D = 128
H = 256
TILES = 4
SUPER = P * TILES
SUPERS = 4
GROUP = SUPER * SUPERS
WIN = 64
CHUNK = 7
LN_EPS = 1e-5

ALU = mybir.AluOpType
ACT = mybir.ActivationFunctionType
AX_X = mybir.AxisListType.X
F32 = mybir.dt.float32
BF16 = mybir.dt.bfloat16
I32 = mybir.dt.int32


def build(nc, x, src, dst, edge_attr, edge_weight, eps, W1, b1, gamma, beta, W2, b2, out):
    N = x.shape[0]
    E = src.shape[0]
    NJ = -(-N // P)
    NP = NJ * P
    full_parts, rest_nodes = N // NJ, N % NJ
    DUMP = NP
    chunks = NJ // CHUNK
    assert NJ % (2 * CHUNK) == 0 and chunks >= 4
    windows = -(-N // WIN)
    G = E // GROUP
    rest = E % GROUP
    assert G >= 2 and rest % TILES == 0 and rest
    tail = [P] * (rest // SUPER) + ([rest % SUPER // TILES] if rest % SUPER else [])
    supers = SUPERS * G + len(tail)
    ROWS = G + 1
    assert ROWS <= P
    widths = [P] * SUPERS

    def view_nodes(t):
        return t.rearrange("(p j) d -> p (j d)", j=NJ)

    def started(value):
        return not isinstance(value, int) or value > 0

    with ExitStack() as ctx:
        def dram(name, shape, dt):
            return nc.dram_tensor(name, shape, dt).ap()

        def sb(name, shape, dt=F32):
            return ctx.enter_context(nc.sbuf_tensor(name, shape, dt))

        def sem(name):
            return ctx.enter_context(nc.semaphore(name))

        h_dram = dram("h_scratch", [NP + WIN, D], F32)
        h2_dram = dram("h2_scratch", [NP, D], F32)
        acc_dram = [dram(f"acc_scratch{t}", [NP + P, D], F32) for t in range(TILES)]
        deg_dram = dram("deg_scratch", [NP], F32)

        X = sb("X", [P, NJ * D])
        src_col = sb("src_col", [P, ROWS * 16])
        rel_col = sb("rel_col", [P, ROWS * 16])
        w_col = sb("w_col", [P, ROWS * 16])
        bases = sb("bases", [1, ROWS * SUPERS], I32)
        ident = sb("ident", [P, P])
        ident_b = sb("ident_b", [P, P], BF16)
        earlier = sb("earlier", [P, P])
        lane = sb("lane", [P, WIN])
        win_node = sb("win_node", [P, windows])
        win_first = sb("win_first", [P, windows])
        dump_col = sb("dump_col", [P, 1])
        ones = sb("ones", [P, P])
        eps_col = sb("eps_col", [P, 1])
        ln_eps = sb("ln_eps", [P, 1])
        W1_sb = sb("W1_sb", [P, H])
        W2_sb = sb("W2_sb", [P, 2, D])
        b1_bc = sb("b1_bc", [P, H])
        b2_bc = sb("b2_bc", [P, D])
        gamma_col = sb("gamma_col", [P, 2])
        beta_col = sb("beta_col", [P, 2])
        flag_f = sb("flag_f", [1, 1])
        flag_i = sb("flag_i", [1, 1], I32)
        spread = sb("spread", [P, 4])
        mv = sb("mv", [P, 2, CHUNK, 2])
        stats = sb("stats", [P, 2, CHUNK, 6])
        std = sb("std", [P, 2, CHUNK])
        rstd = sb("rstd", [P, 2, CHUNK])
        nmr = sb("nmr", [P, 2, CHUNK])
        mv2 = sb("mv2", [P, CHUNK, 2])
        stats2 = sb("stats2", [P, CHUNK, 6])
        std2 = sb("std2", [P, CHUNK])
        rstd2 = sb("rstd2", [P, CHUNK])
        nmr2 = sb("nmr2", [P, CHUNK])
        deg_nodes = sb("deg_nodes", [P, NJ])

        aggT_words = NP + WIN
        nodes_words = CHUNK * (2 * TILES * D + 2 * H + 2 * D) + 2 * D + 4 * P
        arena_words = max(nodes_words, aggT_words) + max(aggT_words, 10240)
        arena = sb("arena", [P, arena_words])
        parts_at = arena_words - 2 * GROUP
        src_hi, src_lo, rel_hi, rel_lo = (
            arena[:, parts_at + n * GROUP // 2:parts_at + (n + 1) * GROUP // 2].bitcast(BF16) for n in range(4))
        place = [0]

        def area(words, restart=False):
            if restart:
                place[0] = 0
            a = arena[:, place[0]:place[0] + words]
            place[0] += words
            assert place[0] <= arena_words
            return a

        dst_i = area(GROUP, True).bitcast(I32)
        src_i = area(GROUP).bitcast(I32)
        w_rows = area(GROUP)
        dst_f = area(GROUP)
        src_f = area(GROUP)
        rel_f = area(GROUP)
        part_i = area(GROUP).bitcast(I32)
        h_out = area(2 * CHUNK * D).rearrange("p (b n) -> p b n", b=2)
        eh_out = area(2 * CHUNK * D).rearrange("p (b n) -> p b n", b=2)
        zeros = area(CHUNK * D)
        ea = area(SUPERS * TILES * D, True).rearrange("p (c t d) -> p c t d", c=SUPERS, t=TILES)
        hwin = area(SUPERS * D).rearrange("p (c d) -> p c d", c=SUPERS)
        onehotT = area(2 * SUPER).rearrange("p (b e) -> p b e", b=2)
        same = area(2 * TILES * P).rearrange("p (b t e) -> p b t e", b=2, t=TILES)
        masked = area(2 * TILES * P).rearrange("p (b t e) -> p b t e", b=2, t=TILES)
        summed = area(2 * TILES * D).rearrange("p (b t d) -> p b t d", b=2, t=TILES)
        before = area(2 * TILES).rearrange("p (b t) -> p b t", b=2)
        dump_or_0 = area(2 * TILES).rearrange("p (b t) -> p b t", b=2)
        scatter_idx = area(SUPERS * TILES).bitcast(I32).rearrange("p (c t) -> p c t", c=SUPERS)
        accs = area(2 * TILES * CHUNK * D, True).rearrange("p (b r n) -> p b r n", b=2, r=TILES)
        nodesT = area(2 * D).rearrange("p (b d) -> p b d", b=2)
        h1 = area(2 * CHUNK * H).rearrange("p (b j f) -> p b j f", b=2, j=CHUNK)
        reluT = area(2 * 2 * P).rearrange("p (b s n) -> p b s n", b=2, s=2)
        h2_out = area(2 * CHUNK * D).rearrange("p (b n) -> p b n", b=2)
        assert place[0] == nodes_words
        deg = area(aggT_words, True)[0:1, :]
        aggT = arena[:, arena_words - aggT_words:]
        gathered = sb("gathered", [P, SUPERS, TILES, D])
        gather_idx = sb("gather_idx", [P, SUPERS, TILES], I32)
        rel_win = sb("rel_win", [P, TILES])
        onehot = sb("onehot", [P, 2, TILES, WIN])
        aggT_chunk = area(2 * CHUNK * P, True).rearrange("p (b j n) -> p b j n", b=2, j=CHUNK)
        h2_in = area(2 * CHUNK * D).rearrange("p (b j d) -> p b j d", b=2, j=CHUNK)
        no_edge = sb("no_edge", [P, NJ])
        base_col = sb("base_col", [P, SUPERS])

        bank = [ctx.enter_context(nc.psum_tensor(f"bank{b}", [P, 512], F32)) for b in range(8)]
        dst_bc, src_bc, gath_ps, sum_ps = bank[0:2], bank[2:4], bank[4:6], bank[6:8]
        nodesT_ps, h1_ps, hnT_ps, mlp_ps = bank[0:2], bank[2:4], bank[4:6], bank[6:8]
        agg_ps, deg_ps = bank[0:2], bank[2:4]

        idx_loaded = sem("idx_loaded")
        idx_zeroed = sem("idx_zeroed")
        const_ready = sem("const_ready")
        weights_loaded = sem("weights_loaded")
        x_zeroed = sem("x_zeroed")
        x_loaded = sem("x_loaded")
        prep = sem("prep")
        REL_MADE, WAY_OUT_MADE, FLAG_MADE, ROWS_MADE, PARTS_MADE = 2, 6, 8, 12, 19
        way_out_turned = sem("way_out_turned")
        flag_spread = sem("flag_spread")
        h_made = sem("h_made")
        eps1_ready = sem("eps1_ready")
        eh_ready = sem("eh_ready")
        sums_added = sem("sums_added")
        pool_turns = sem("pool_turns")
        dve_turns = sem("dve_turns")
        rel_cut = sem("rel_cut")
        flag_ready = sem("flag_ready")
        col_turned = sem("col_turned")
        col_ready = sem("col_ready")
        zeros_ready = sem("zeros_ready")
        cleared = sem("cleared")
        ln_stats = sem("ln_stats")
        ln_mv = sem("ln_mv")
        ln_std = sem("ln_std")
        ln_rstd = sem("ln_rstd")
        ln_nmr = sem("ln_nmr")
        h_stored = [sem(f"h_stored{b}") for b in range(2)]
        eh_stored = [sem(f"eh_stored{b}") for b in range(2)]
        ea_landed = [sem(f"ea_landed{c}") for c in range(SUPERS)]
        hwin_landed = [sem(f"hwin_landed{c}") for c in range(SUPERS)]
        dst_spread = sem("dst_spread")
        src_spread = sem("src_spread")
        onehotT_ready = sem("onehotT_ready")
        h_gathered = sem("h_gathered")
        h_added = sem("h_added")
        message_ready = sem("message_ready")
        same_ready = sem("same_ready")
        before_ready = sem("before_ready")
        dump_ready = sem("dump_ready")
        scatter_idx_ready = sem("scatter_idx_ready")
        merged = sem("merged")
        summed_ready = sem("summed_ready")
        scattered = [sem(f"scattered{t}") for t in range(TILES)]
        accs_landed = [sem(f"accs_landed{b}") for b in range(2)]
        pool_summed = sem("pool_summed")
        half_summed = sem("half_summed")
        nodes_ready = sem("nodes_ready")
        nodes_turned = sem("nodes_turned")
        nodesT_ready = sem("nodesT_ready")
        h1_done = sem("h1_done")
        h1_ready = sem("h1_ready")
        mlp_stats = sem("mlp_stats")
        mlp_mv = sem("mlp_mv")
        mlp_std = sem("mlp_std")
        mlp_rstd = sem("mlp_rstd")
        mlp_nmr = sem("mlp_nmr")
        hn_ready = sem("hn_ready")
        hn_turned = sem("hn_turned")
        reluT_ready = sem("reluT_ready")
        mlp_done = sem("mlp_done")
        b2_added = sem("b2_added")
        x1_ready = sem("x1_ready")
        ln2_stats = sem("ln2_stats")
        ln2_mv = sem("ln2_mv")
        ln2_std = sem("ln2_std")
        ln2_rstd = sem("ln2_rstd")
        ln2_nmr = sem("ln2_nmr")
        h2_ready = sem("h2_ready")
        h2_stored = [sem(f"h2_stored{b}") for b in range(2)]
        agg_zeroed = sem("agg_zeroed")
        deg_zeroed = sem("deg_zeroed")
        gather_idx_ready = sem("gather_idx_ready")
        gathered_landed = [sem(f"gathered_landed{c}") for c in range(SUPERS)]
        weighted = sem("weighted")
        rel_shifted = sem("rel_shifted")
        onehot_ready = sem("onehot_ready")
        agg_done = sem("agg_done")
        agg_added = sem("agg_added")
        deg_stored = sem("deg_stored")
        deg_loaded = sem("deg_loaded")
        no_edge_ready = sem("no_edge_ready")
        h2_loaded = [sem(f"h2_loaded{b}") for b in range(2)]
        agg_copied = sem("agg_copied")
        agg_turned = sem("agg_turned")
        agg_out = sem("agg_out")
        own_ready = sem("own_ready")
        result_ready = sem("result_ready")
        stored = sem("stored")

        CONSTS = 11
        WEIGHTS = 7

        def part_cuts(n):
            cut = n // 16 * 16
            return [(a, b) for a, b in ((0, cut), (cut, n)) if b > a]

        node_cuts = [(a, b, NJ) for a, b in part_cuts(full_parts)]
        if rest_nodes:
            node_cuts.append((full_parts, full_parts + 1, rest_nodes))
        row_cuts = [(a, b, GROUP) for a, b in part_cuts(G)] + [(G, G + 1, rest)]

        def both_ways(eng, program):
            fast = eng.value_load(flag_i[0:1, 0:1], min_val=0, max_val=1)
            with eng.If(fast):
                program(1)
            with eng.Else():
                program(windows)

        def over_groups(eng, group):
            group(0, widths)
            with eng.Fori(1, G) as k:
                group(k, widths)
            group(G, tail)

        def over_chunks(eng, pair):
            pair(0)
            if chunks > 2:
                with eng.Fori(1, chunks // 2) as m:
                    pair(m)

        def over_windows(eng, nw, step):
            if nw == 1:
                step(0)
            else:
                with eng.Fori(0, nw) as w:
                    step(w)

        def cols(i):
            return bass.ds(TILES * i, TILES)

        block = ctx.enter_context(nc.Block())

        @block.sync
        def _(sp):
            sp.wait_ge(idx_zeroed, 3)
            for rows, of in ((dst_i, dst), (src_i, src), (w_rows, edge_weight)):
                for a, b, n in row_cuts:
                    sp.dma_start(rows[a:b, 0:n], of[a * GROUP:a * GROUP + (b - a) * n].rearrange(
                        "(k e) -> k e", e=n)).then_inc(idx_loaded, 16)
            with nc.allow_non_contiguous_dma(reason="one dst of each supertile, once"):
                nb = -(-E // SUPER)
                sp.dma_start(bases[0:1, 0:nb - 1], dst[0:(nb - 1) * SUPER].rearrange(
                    "(a s e) -> a s e", a=1, e=SUPER)[:, :, 0]).then_inc(idx_loaded, 16)
                sp.dma_start(bases[0:1, nb - 1:nb], dst[(nb - 1) * SUPER:(nb - 1) * SUPER + 1].rearrange(
                    "(a s) -> a s", a=1)).then_inc(idx_loaded, 16)
                sp.dma_start(gamma_col[:, :], gamma.rearrange("(s p) -> p s", p=P)).then_inc(weights_loaded, 16)
                sp.dma_start(beta_col[:, :], beta.rearrange("(s p) -> p s", p=P)).then_inc(weights_loaded, 16)
            sp.wait_ge(x_zeroed, 1)
            for a, b, n in node_cuts:
                sp.dma_start(X[a:b, 0:n * D], x[a * NJ:a * NJ + (b - a) * n, :].rearrange(
                    "(p j) d -> p (j d)", j=n)).then_inc(x_loaded, 16)
            sp.dma_start(W1_sb[:, :], W1).then_inc(weights_loaded, 16)
            sp.dma_start(W2_sb[:, :, :], W2.rearrange("(s p) d -> p s d", p=P)).then_inc(weights_loaded, 16)
            for row, of in ((b1_bc, b1), (b2_bc, b2), (eps_col, eps)):
                sp.dma_start(row[:, :], of.rearrange("(a n) -> a n", a=1).to_broadcast(row.shape)).then_inc(
                    weights_loaded, 16)

            def store_h(m):
                for b in range(2):
                    q = 2 * m + b
                    sp.wait_ge(h_made, q + 1)
                    sp.wait_ge(eh_ready, q + 1)
                    at = bass.ds(q * CHUNK * D, CHUNK * D)
                    sp.dma_start(view_nodes(h_dram[0:NP, :])[:, at], h_out[:, b, :]).then_inc(h_stored[b], 16)
                    sp.dma_start(view_nodes(acc_dram[0][0:NP, :])[:, at], eh_out[:, b, :]).then_inc(
                        eh_stored[b], 16)

            over_chunks(sp, store_h)

            for b in range(2):
                sp.wait_ge(h_stored[b], 16 * (chunks // 2))
                sp.wait_ge(eh_stored[b], 16 * (chunks // 2))
            sp.wait_ge(cleared, 16 * 2 * TILES)
            sp.wait_ge(flag_ready, 1)
            sp.wait_ge(prep, PARTS_MADE)
            sp.wait_ge(col_ready, 3 * SUPERS)

            def loads(nw):
                def group(k, parts):
                    for c, n in enumerate(parts):
                        i = SUPERS * k + c
                        if started(k):
                            sp.wait_ge(merged, i - SUPERS + 1)
                        sp.dma_start(ea[0:n, c, :, :], edge_attr[bass.ds(SUPER * i, n * TILES), :].rearrange(
                            "(p t) d -> p t d", t=TILES)).then_inc(ea_landed[c], 16)

                        def window(w):
                            step = i * nw + w
                            last = i - SUPERS + 1 if nw == 1 else step
                            if started(last):
                                sp.wait_ge(h_gathered, last)
                            if nw == 1:
                                base = sp.value_load(bases[0:1, bass.ds(i, 1)], min_val=0, max_val=N - 1)
                            else:
                                base = w * WIN
                            sp.dma_start(hwin[0:WIN, c, :], h_dram[bass.ds(base, WIN), :]).then_inc(
                                hwin_landed[c], 16)

                        over_windows(sp, nw, window)

                over_groups(sp, group)

            both_ways(sp, loads)

            for t in range(TILES):
                sp.wait_ge(scattered[t], 16 * supers)

            def load_accs(b, q):
                if started(CHUNK * (q - 1)):
                    sp.wait_ge(nodes_turned, CHUNK * (q - 1))
                for t in range(TILES):
                    sp.dma_start(accs[:, b, t, :], view_nodes(acc_dram[t][0:NP, :])[
                        :, bass.ds(q * CHUNK * D, CHUNK * D)]).then_inc(accs_landed[b], 16)

            def store_h2(b, q):
                sp.wait_ge(h2_ready, CHUNK * (q + 1))
                sp.dma_start(view_nodes(h2_dram)[:, bass.ds(q * CHUNK * D, CHUNK * D)], h2_out[:, b, :]).then_inc(
                    h2_stored[b], 16)

            for q in range(4):
                load_accs(q % 2, q)
            if chunks > 4:
                with sp.Fori(2, chunks // 2) as m:
                    for b in range(2):
                        load_accs(b, 2 * m + b)
                        store_h2(b, 2 * m - 4 + b)
            for q in range(chunks - 4, chunks):
                store_h2(q % 2, q)

            sp.wait_ge(agg_added, 1)
            sp.dma_start(deg_dram.rearrange("(a n) -> a n", a=1), deg[:, 0:NP]).then_inc(deg_stored, 16)
            sp.wait_ge(deg_stored, 16)
            sp.dma_start(deg_nodes[:, :], deg_dram.rearrange("(p j) -> p j", j=NJ)).then_inc(deg_loaded, 16)

            def load_h2(b, q):
                if started(q - 1):
                    sp.wait_ge(result_ready, q - 1)
                sp.dma_start(h2_in[:, b, :, :], h2_dram.rearrange("(p j) d -> p j d", j=NJ)[
                    :, bass.ds(q * CHUNK, CHUNK), :]).then_inc(h2_loaded[b], 16)

            def store_result(m):
                sp.wait_ge(result_ready, 2 * (m + 1))
                at = bass.ds(m * 2 * CHUNK * D, 2 * CHUNK * D)
                for a, b in part_cuts(full_parts):
                    sp.dma_start(out[a * NJ:b * NJ, :].rearrange("(p j) d -> p (j d)", j=NJ)[:, at],
                                 X[a:b, at]).then_inc(stored, 16)

            for b in range(2):
                load_h2(b, b)
            with sp.Fori(1, chunks // 2) as m:
                for b in range(2):
                    load_h2(b, 2 * m + b)
                store_result(m - 1)
            store_result(chunks // 2 - 1)
            if rest_nodes:
                sp.dma_start(out[full_parts * NJ:N, :].rearrange("(p j) d -> p (j d)", p=1),
                             X[full_parts:full_parts + 1, 0:rest_nodes * D]).then_inc(stored, 16)
            sp.wait_ge(stored, 16 * (len(part_cuts(full_parts)) * chunks // 2 + (rest_nodes > 0)))


        @block.gpsimd
        def _(pool):
            for rows in (dst_i, src_i, w_rows):
                nc.gpsimd.memset(rows, 0).then_inc(idx_zeroed, 1)
            nc.gpsimd.memset(zeros, 0.0).then_inc(zeros_ready, 1)
            nc.gpsimd.memset(ident[:, :], 0.0).then_inc(const_ready, 1)
            nc.gpsimd.memset(earlier[:, :], 1.0).then_inc(const_ready, 1)
            nc.gpsimd.memset(ones[:, :], 1.0).then_inc(const_ready, 1)
            nc.gpsimd.memset(ln_eps[:, :], LN_EPS).then_inc(const_ready, 1)
            nc.gpsimd.iota(lane[:, :], pattern=[[1, WIN]], base=0, channel_multiplier=0,
                           allow_small_or_imprecise_dtypes=True).then_inc(const_ready, 1)
            nc.gpsimd.iota(win_node[:, :], pattern=[[WIN, windows]], base=0, channel_multiplier=1,
                           allow_small_or_imprecise_dtypes=True).then_inc(const_ready, 1)
            nc.gpsimd.iota(win_first[:, :], pattern=[[WIN, windows]], base=0, channel_multiplier=0,
                           allow_small_or_imprecise_dtypes=True).then_inc(const_ready, 1)
            nc.gpsimd.iota(dump_col[:, :], pattern=[[0, 1]], base=DUMP, channel_multiplier=1,
                           allow_small_or_imprecise_dtypes=True).then_inc(const_ready, 1)
            pool.wait_ge(const_ready, 8)
            nc.gpsimd.affine_select(out=ident[:, :], in_=ident[:, :], compare_op=ALU.not_equal, fill=1.0,
                                    base=0, pattern=[[-1, P]], channel_multiplier=1).then_inc(const_ready, 1)
            nc.gpsimd.affine_select(out=earlier[:, :], in_=earlier[:, :], compare_op=ALU.is_ge, fill=0.0,
                                    base=-1, pattern=[[-1, P]], channel_multiplier=1).then_inc(const_ready, 1)
            pool.wait_ge(const_ready, 10)
            nc.gpsimd.tensor_copy(ident_b[:, :], ident[:, :]).then_inc(const_ready, 1)
            pool.wait_ge(prep, REL_MADE)
            nc.gpsimd.affine_select(out=rel_f, in_=rel_f, compare_op=ALU.is_ge, fill=0.0, base=E - 1,
                                    pattern=[[-1, GROUP]], channel_multiplier=-GROUP).then_inc(rel_cut, 1)

            pool.wait_ge(eps1_ready, 1)

            def scale_h(m):
                for b in range(2):
                    q = 2 * m + b
                    pool.wait_ge(h_made, q + 1)
                    if started(m):
                        pool.wait_ge(eh_stored[b], 16 * m)
                    pool.sem_inc(pool_turns, 1)
                    nc.gpsimd.tensor_scalar(eh_out[:, b, :], h_out[:, b, :], eps_col[:, 0:1], None,
                                            ALU.mult).then_inc(eh_ready, 1)

            over_chunks(pool, scale_h)

            pool.wait_ge(cleared, 16 * 2 * TILES)
            for b in range(2):
                pool.wait_ge(eh_stored[b], 16 * (chunks // 2))

            def scatter(k, parts):
                for c, n in enumerate(parts):
                    i = SUPERS * k + c
                    pool.wait_ge(scatter_idx_ready, i + 1)
                    pool.wait_ge(summed_ready, i + 1)
                    for t in range(TILES):
                        if started(i):
                            pool.wait_ge(scattered[t], 16 * i)
                        pool.sem_inc(pool_turns, 1)
                        nc.gpsimd.indirect_dma_start(
                            acc_dram[t], bass.IndirectOffsetOnAxis(scatter_idx[0:n, c, t:t + 1], 0),
                            summed[0:n, c % 2, t, :], None, compute_op=ALU.add).then_inc(scattered[t], 16)

            over_groups(pool, scatter)

            def sum_half(b, m):
                pool.wait_ge(accs_landed[b], 16 * TILES * (m + 1))
                nc.gpsimd.tensor_tensor(accs[:, b, 2, :], accs[:, b, 2, :], accs[:, b, 3, :], ALU.add).then_inc(
                    pool_summed, 1)

            def norm(b, q):
                pool.wait_ge(mlp_nmr, q + 1)
                pool.sem_inc(pool_turns, 1)
                for j in range(CHUNK):
                    nc.gpsimd.tensor_scalar(h1[:, b, j, :], h1[:, b, j, :], rstd[:, b, j:j + 1],
                                            nmr[:, b, j:j + 1], ALU.mult, ALU.add).then_inc(hn_ready, 1)

            def add_b2(b, q):
                at = bass.ds(q * CHUNK * D, CHUNK * D)
                nc.gpsimd.tensor_tensor(
                    X[:, at].rearrange("p (j d) -> p j d", d=D), X[:, at].rearrange("p (j d) -> p j d", d=D),
                    b2_bc[:, :].rearrange("p (a d) -> p a d", a=1).to_broadcast([P, CHUNK, D]),
                    ALU.add).then_inc(b2_added, 1)

            def pair(m):
                sum_half(0, m)
                add_b2(0, 2 * m)
                if not started(m):
                    nc.gpsimd.memset(aggT, 0.0).then_inc(agg_zeroed, 1)
                if started(m):
                    norm(1, 2 * m - 1)
                sum_half(1, m)
                add_b2(1, 2 * m + 1)
                norm(0, 2 * m)

            over_chunks(pool, pair)
            norm(1, chunks - 1)

            for b in range(2):
                pool.wait_ge(h2_stored[b], 16 * (chunks // 2))

            def gathers(nw):
                def group(k, parts):
                    for c, n in enumerate(parts):
                        i = SUPERS * k + c
                        pool.wait_ge(gather_idx_ready, i + 1)
                        if started(i - SUPERS + 1):
                            pool.wait_ge(agg_done, (i - SUPERS + 1) * nw)
                        pool.sem_inc(pool_turns, 1)
                        for t in range(TILES):
                            nc.gpsimd.indirect_dma_start(
                                gathered[0:n, c, t, :], None, h2_dram,
                                bass.IndirectOffsetOnAxis(gather_idx[0:n, c, t:t + 1], 0)).then_inc(gathered_landed[c], 16)

                over_groups(pool, group)

            both_ways(pool, gathers)

            pool.wait_ge(no_edge_ready, 1)

            def own(m):
                for b in range(2):
                    q = 2 * m + b
                    pool.wait_ge(h2_loaded[b], 16 * (m + 1))
                    nc.gpsimd.tensor_tensor(
                        h2_in[:, b, :, :], h2_in[:, b, :, :],
                        no_edge[:, bass.ds(q * CHUNK, CHUNK)].rearrange("p (j a) -> p j a", a=1).to_broadcast(
                            [P, CHUNK, D]), ALU.mult).then_inc(own_ready, 1)

            over_chunks(pool, own)

        @block.tensor
        def _(pe):
            pe.wait_ge(const_ready, CONSTS)
            pe.wait_ge(prep, WAY_OUT_MADE)
            nc.tensor.transpose(bank[0][0:1, 0:P], spread[:, 3:4], ident[:, :]).then_inc(way_out_turned, 1)
            pe.wait_ge(prep, FLAG_MADE)
            nc.tensor.matmul(bank[1][:, 0:1], ones[0:1, :], flag_f[:, :], start=True, stop=True).then_inc(
                flag_spread, 1)
            pe.wait_ge(prep, ROWS_MADE)
            n = 0
            for rows in (src_f, rel_f, w_rows):
                for c in range(SUPERS):
                    if n >= 2:
                        pe.wait_ge(col_ready, n - 1)
                    for t in range(TILES):
                        last = nc.tensor.transpose(bank[2 + n % 2][:, t * P:(t + 1) * P],
                                                   rows[:, c * SUPER + t:(c + 1) * SUPER:TILES], ident[:, :])
                    last.then_inc(col_turned, 1)
                    n += 1

            pe.wait_ge(flag_ready, 1)
            pe.wait_ge(prep, PARTS_MADE)
            pe.wait_ge(col_ready, 3 * SUPERS)

            def edges(nw):
                def spread_rows(k, c, i):
                    b = c % 2
                    pick = ident_b[:, bass.ds(k, 1)].to_broadcast([P, P])
                    e = slice(c * SUPER, (c + 1) * SUPER)
                    if started((i - 1) * nw):
                        pe.wait_ge(onehotT_ready, (i - 1) * nw)
                    nc.tensor.matmul(dst_bc[b][:, :], pick, rel_hi[:, e], start=True, stop=False)
                    nc.tensor.matmul(dst_bc[b][:, :], pick, rel_lo[:, e], start=False, stop=True).then_inc(
                        dst_spread, 1)
                    if started(i - 1):
                        pe.wait_ge(same_ready, i - 1)
                    nc.tensor.matmul(src_bc[b][:, :], pick, src_hi[:, e], start=True, stop=False)
                    nc.tensor.matmul(src_bc[b][:, :], pick, src_lo[:, e], start=False, stop=True).then_inc(
                        src_spread, 1)

                def gather(k, c, n, i):
                    b = c % 2

                    def window(w):
                        step = i * nw + w
                        pe.wait_ge(onehotT_ready, step + 1)
                        pe.wait_ge(hwin_landed[c], 16 * (k * nw + w + 1))
                        last = i - 1 if nw == 1 else step
                        if started(last):
                            pe.wait_ge(h_added, last)
                        for t in range(TILES):
                            mm = nc.tensor.matmul(gath_ps[b][0:n, t * D:(t + 1) * D],
                                                  onehotT[0:WIN, b, t:n * TILES:TILES], hwin[0:WIN, c, :],
                                                  start=True, stop=True)
                        mm.then_inc(h_gathered, 1)

                    over_windows(pe, nw, window)

                def merge(c, n, i):
                    b = c % 2
                    pe.wait_ge(same_ready, i + 1)
                    pe.wait_ge(message_ready, i + 1)
                    if started(i - 1):
                        pe.wait_ge(summed_ready, i - 1)
                    for t in range(TILES):
                        mm = nc.tensor.matmul(sum_ps[b][0:n, t * D:(t + 1) * D], same[0:n, b, t, 0:n],
                                              ea[0:n, c, t, :], start=True, stop=True)
                    mm.then_inc(merged, 1)

                def group(k, parts, following):
                    for c, n in enumerate(parts):
                        i = SUPERS * k + c
                        ahead = (k, c + 1, parts[c + 1]) if c + 1 < len(parts) else following
                        if ahead:
                            spread_rows(ahead[0], ahead[1], i + 1)
                        merge(c, n, i)
                        if ahead:
                            gather(*ahead, i + 1)

                spread_rows(0, 0, 0)
                gather(0, 0, P, 0)
                group(0, widths, (1, 0, P))
                with pe.Fori(1, G) as k:
                    group(k, widths, (k + 1, 0, P))
                group(G, tail, None)

            both_ways(pe, edges)

            for t in range(TILES):
                pe.wait_ge(scattered[t], 16 * supers)
            pe.wait_ge(weights_loaded, 16 * WEIGHTS)

            def turn_nodes(b, q, j):
                n = CHUNK * q + j
                s = (CHUNK * b + j) % 2
                if started(n - 1):
                    pe.wait_ge(nodesT_ready, n - 1)
                nc.tensor.transpose(nodesT_ps[s][:, 0:P], accs[:, b, 0, j * D:(j + 1) * D],
                                    ident[:, :]).then_inc(nodes_turned, 1)

            def first_product(b, q, j):
                n = CHUNK * q + j
                s = (CHUNK * b + j) % 2
                pe.wait_ge(nodesT_ready, n + 1)
                if started(n - 1):
                    pe.wait_ge(h1_ready, n - 1)
                nc.tensor.matmul(h1_ps[s][:, 0:H], nodesT[:, s, :], W1_sb[:, :], start=True,
                                 stop=True).then_inc(h1_done, 1)

            def turn_hn(b, q, j):
                n = CHUNK * q + j
                s = (CHUNK * b + j) % 2
                pe.wait_ge(hn_ready, n + 1)
                if started(n - 1):
                    pe.wait_ge(reluT_ready, 2 * (n - 1))
                for half in range(2):
                    turn = nc.tensor.transpose(hnT_ps[s][:, half * P:(half + 1) * P],
                                               h1[:, b, j, half * P:(half + 1) * P], ident[:, :])
                turn.then_inc(hn_turned, 1)

            def second_product(b, q, j):
                n = CHUNK * q + j
                s = (CHUNK * b + j) % 2
                pe.wait_ge(reluT_ready, 2 * (n + 1))
                if started(n - 1):
                    pe.wait_ge(x1_ready, n - 1)
                for half in range(2):
                    mm = nc.tensor.matmul(mlp_ps[s][:, 0:D], reluT[:, s, half, :], W2_sb[:, half, :],
                                          start=half == 0, stop=half == 1)
                mm.then_inc(mlp_done, 1)

            def chunk(b, q, first=True, second=True):
                if first:
                    pe.wait_ge(nodes_ready, q + 1)
                    turn_nodes(b, q, 0)
                if second and first:
                    turn_nodes(b, q, 1)
                    first_product(b, q, 0)
                if second:
                    turn_hn(1 - b, q - 1, 0)
                for j in range(CHUNK):
                    if first and j + 1 < CHUNK and (j or not second):
                        turn_nodes(b, q, j + 1)
                    if second and j + 1 < CHUNK:
                        turn_hn(1 - b, q - 1, j + 1)
                    if first and (j or not second):
                        first_product(b, q, j)
                    if second:
                        second_product(1 - b, q - 1, j)

            def pair(m):
                chunk(0, 2 * m, second=started(m))
                chunk(1, 2 * m + 1)

            over_chunks(pe, pair)
            chunk(0, chunks, first=False)

            def sums(nw):
                def group(k, parts):
                    for c, n in enumerate(parts):
                        i = SUPERS * k + c
                        b = c % 2

                        def window(w):
                            step = i * nw + w
                            pe.wait_ge(weighted, i + 1)
                            pe.wait_ge(onehot_ready, step + 1)
                            last = step - 1 if nw == 1 else step
                            if started(last):
                                pe.wait_ge(sums_added, 2 * last)
                            for t in range(TILES):
                                nc.tensor.matmul(agg_ps[b][:, 0:WIN], gathered[0:n, c, t, :], onehot[0:n, b, t, :],
                                                 start=t == 0, stop=t == TILES - 1)
                            for t in range(TILES):
                                mm = nc.tensor.matmul(deg_ps[b][0:1, 0:WIN], ones[0:n, 0:1], onehot[0:n, b, t, :],
                                                      start=t == 0, stop=t == TILES - 1)
                            mm.then_inc(agg_done, 1)

                        over_windows(pe, nw, window)

                over_groups(pe, group)

            both_ways(pe, sums)

            pe.wait_ge(agg_added, 1)

            def turns(m):
                for b in range(2):
                    q = 2 * m + b
                    pe.wait_ge(agg_copied, q + 1)
                    if started(q - 1):
                        pe.wait_ge(agg_out, 2 * (q - 1))
                    for j in range(CHUNK):
                        turn = nc.tensor.transpose(bank[4 + 2 * b + j // 4][:, j % 4 * D:j % 4 * D + D],
                                                   aggT_chunk[:, b, j, :], ident[:, :])
                    turn.then_inc(agg_turned, 1)

            over_chunks(pe, turns)

        @block.scalar
        def _(act):
            act.wait_ge(zeros_ready, 1)
            act.wait_ge(x_loaded, 16 * len(node_cuts))
            for t in range(TILES):
                if t:
                    act.dma_start(
                        acc_dram[t][0:NP, :].rearrange("(p q n) d -> p q (n d)", p=P, q=chunks),
                        zeros[:, :].rearrange("p (a n) -> p a n", a=1).to_broadcast([P, chunks, CHUNK * D]),
                    ).then_inc(cleared, 16)
                act.dma_start(acc_dram[t][DUMP:DUMP + P, :], zeros[:, 0:D]).then_inc(cleared, 16)
            act.dma_start(h_dram[NP:NP + WIN, :], zeros[0:WIN, 0:D]).then_inc(cleared, 16)

            n = 0
            for col in (src_col, rel_col, w_col):
                for c in range(SUPERS):
                    act.wait_ge(col_turned, n + 1)
                    nc.scalar.copy(
                        col[:, :].rearrange("p (k c t) -> p c t k", c=SUPERS, t=TILES)[:, c, :, :],
                        bank[2 + n % 2][:, :].rearrange("p (t k) -> p t k", t=TILES)[:, :, 0:ROWS],
                    ).then_inc(col_ready, 1)
                    n += 1

            act.wait_ge(const_ready, CONSTS)
            act.wait_ge(weights_loaded, 16 * WEIGHTS)

            def norm_x(m):
                for b in range(2):
                    q = 2 * m + b
                    act.wait_ge(ln_mv, CHUNK * (q + 1))
                    nc.scalar.activation(std[:, b, :], mv[:, b, :, 1], ACT.Sqrt, bias=ln_eps[:, 0:1]).then_inc(
                        ln_std, 1)
                    act.wait_ge(ln_nmr, q + 1)
                    if started(m):
                        act.wait_ge(h_stored[b], 16 * m)
                        act.wait_ge(eh_stored[b], 16 * m)
                    for j in range(CHUNK):
                        last = nc.scalar.activation(h_out[:, b, j * D:(j + 1) * D],
                                                    X[:, bass.ds((q * CHUNK + j) * D, D)], ACT.Relu,
                                                    scale=rstd[:, b, j:j + 1], bias=nmr[:, b, j:j + 1])
                    last.then_inc(h_made, 1)

            over_chunks(act, norm_x)

            act.wait_ge(flag_ready, 1)
            for b in range(2):
                act.wait_ge(h_stored[b], 16 * (chunks // 2))

            def messages(nw):
                def group(k, parts):
                    for c, n in enumerate(parts):
                        i = SUPERS * k + c
                        b = c % 2
                        act.wait_ge(h_added, (i + 1) * nw)
                        nc.scalar.activation(ea[0:n, c, :, :], ea[0:n, c, :, :], ACT.Relu).then_inc(message_ready, 1)
                        act.wait_ge(merged, i + 1)
                        if started(i - 1):
                            for t in range(TILES):
                                act.wait_ge(scattered[t], 16 * (i - 1))
                        nc.scalar.copy(summed[0:n, b, :, :], sum_ps[b][0:n, :].rearrange(
                            "p (t d) -> p t d", t=TILES)).then_inc(summed_ready, 1)

                over_groups(act, group)

            both_ways(act, messages)

            for t in range(TILES):
                act.wait_ge(scattered[t], 16 * supers)

            def turned_nodes(b, q, j):
                n = CHUNK * q + j
                s = (CHUNK * b + j) % 2
                act.wait_ge(nodes_turned, n + 1)
                if started(n - 1):
                    act.wait_ge(h1_done, n - 1)
                nc.scalar.copy(nodesT[:, s, :], nodesT_ps[s][:, 0:P]).then_inc(nodesT_ready, 1)

            def turned_hn(b, q, j):
                n = CHUNK * q + j
                s = (CHUNK * b + j) % 2
                act.wait_ge(hn_turned, n + 1)
                if started(n - 1):
                    act.wait_ge(mlp_done, n - 1)
                for half in range(2):
                    nc.scalar.activation(reluT[:, s, half, :], hnT_ps[s][:, half * P:(half + 1) * P], ACT.Relu,
                                         scale=gamma_col[:, half:half + 1],
                                         bias=beta_col[:, half:half + 1]).then_inc(reluT_ready, 1)

            def second_norm(q):
                act.wait_ge(ln2_mv, CHUNK * (q + 1))
                nc.scalar.activation(std2[:, :], mv2[:, :, 1], ACT.Sqrt, bias=ln_eps[:, 0:1]).then_inc(ln2_std, 1)

            def make_h2(b, q, m, j):
                if j == 0:
                    act.wait_ge(ln2_nmr, q + 1)
                    if started(m):
                        act.wait_ge(h2_stored[b], 16 * m)
                nc.scalar.activation(h2_out[:, b, j * D:(j + 1) * D], X[:, bass.ds((q * CHUNK + j) * D, D)],
                                     ACT.Relu, scale=rstd2[:, j:j + 1], bias=nmr2[:, j:j + 1]).then_inc(h2_ready, 1)

            def chunk(b, q, m, first=True, second=True, third=True):
                if first:
                    turned_nodes(b, q, 0)
                if first and second:
                    turned_nodes(b, q, 1)
                if second:
                    turned_hn(1 - b, q - 1, 0)
                for j in range(CHUNK):
                    if first and j + 1 < CHUNK and (j or not second):
                        turned_nodes(b, q, j + 1)
                    if second and j + 1 < CHUNK:
                        turned_hn(1 - b, q - 1, j + 1)
                    if third:
                        make_h2(b, q - 2, m, j)
                if first:
                    act.wait_ge(mlp_mv, CHUNK * (q + 1))
                    nc.scalar.activation(std[:, b, :], mv[:, b, :, 1], ACT.Sqrt, bias=ln_eps[:, 0:1]).then_inc(
                        mlp_std, 1)
                if second:
                    second_norm(q - 1)

            def pair(m):
                chunk(0, 2 * m, m - 1, second=started(m), third=started(m))
                chunk(1, 2 * m + 1, m - 1, third=started(m))

            over_chunks(act, pair)
            chunk(0, chunks, chunks // 2 - 1, first=False)
            for j in range(CHUNK):
                make_h2(1, chunks - 1, chunks // 2 - 1, j)

            for b in range(2):
                act.wait_ge(h2_stored[b], 16 * (chunks // 2))

            def indices(k, parts):
                for c, n in enumerate(parts):
                    i = SUPERS * k + c
                    if started(k):
                        act.wait_ge(gathered_landed[c], 16 * TILES * k)
                    nc.scalar.copy(gather_idx[0:n, c, :], src_col[0:n, cols(i)]).then_inc(gather_idx_ready, 1)

            indices(0, widths)
            nc.scalar.copy(deg, win_first[0:1, 0:1].to_broadcast([1, aggT_words])).then_inc(deg_zeroed, 1)
            with act.Fori(1, G) as k:
                indices(k, widths)
            indices(G, tail)

            act.wait_ge(agg_added, 1)
            act.wait_ge(deg_stored, 16)
            sums = aggT[:, 0:NP].rearrange("f (p j) -> f j p", j=NJ)

            def copies(m):
                for b in range(2):
                    q = 2 * m + b
                    if started(q - 1):
                        act.wait_ge(agg_turned, q - 1)
                    nc.scalar.copy(aggT_chunk[:, b, :, :], sums[:, bass.ds(q * CHUNK, CHUNK), :]).then_inc(
                        agg_copied, 1)

            over_chunks(act, copies)

        @block.vector
        def _(dve):
            done = [0]

            def prep_step(ins):
                ins.then_inc(prep, 1)
                done[0] += 1
                dve.wait_ge(prep, done[0])

            def by_super(rows):
                return rows.rearrange("p (c e) -> p c e", c=SUPERS)

            nc.vector.memset(X[96:P, min(rest_nodes, NJ - 1) * D:], 0.0).then_inc(x_zeroed, 1)

            dve.wait_ge(idx_loaded, 16 * (3 * len(row_cuts) + 2))
            dve.wait_ge(const_ready, CONSTS)
            prep_step(nc.vector.tensor_copy(dst_f, dst_i))
            first = by_super(dst_f)[:, :, 0:1]
            prep_step(nc.vector.tensor_tensor(by_super(rel_f), by_super(dst_f),
                                              first.to_broadcast([P, SUPERS, SUPER]), ALU.subtract))
            dve.wait_ge(rel_cut, 1)
            prep_step(nc.vector.tensor_reduce(spread[:, 0:1], rel_f, AX_X, ALU.max))
            prep_step(nc.vector.tensor_reduce(spread[:, 1:2], rel_f, AX_X, ALU.min))
            prep_step(nc.vector.tensor_scalar(spread[:, 2:3], spread[:, 0:1], float(1 - WIN), None, ALU.add))
            prep_step(nc.vector.scalar_tensor_tensor(out=spread[:, 3:4], in0=spread[:, 1:2], scalar=-1.0,
                                                     in1=spread[:, 2:3], op0=ALU.mult, op1=ALU.max))
            assert done[0] == WAY_OUT_MADE
            dve.wait_ge(way_out_turned, 1)
            prep_step(nc.vector.tensor_reduce(spread[0:1, 0:1], bank[0][0:1, 0:P], AX_X, ALU.max))
            prep_step(nc.vector.tensor_scalar(flag_f[:, :], spread[0:1, 0:1], 0.0, None, ALU.is_le))
            assert done[0] == FLAG_MADE
            nc.vector.tensor_copy(flag_i[:, :], flag_f[:, :]).then_inc(flag_ready, 1)
            dve.wait_ge(flag_spread, 1)
            prep_step(nc.vector.tensor_copy(spread[:, 2:3], bank[1][:, 0:1]))
            prep_step(nc.vector.tensor_scalar(base_col[:, :], first.rearrange("p c a -> p (c a)"), spread[:, 2:3],
                                              None, ALU.mult))
            prep_step(nc.vector.tensor_tensor(
                by_super(rel_f), by_super(dst_f),
                base_col[:, :].rearrange("p (c a) -> p c a", a=1).to_broadcast([P, SUPERS, SUPER]), ALU.subtract))
            prep_step(nc.vector.tensor_copy(src_f, src_i))
            assert done[0] == ROWS_MADE
            prep_step(nc.vector.tensor_single_scalar(part_i, src_i, WIN - 1, op=ALU.bitwise_and))
            prep_step(nc.vector.tensor_tensor(src_hi, src_f, part_i, ALU.subtract))
            prep_step(nc.vector.tensor_copy(src_lo, part_i))
            prep_step(nc.vector.tensor_copy(dst_i, rel_f))
            prep_step(nc.vector.tensor_single_scalar(part_i, dst_i, WIN - 1, op=ALU.bitwise_and))
            prep_step(nc.vector.tensor_tensor(rel_hi, rel_f, part_i, ALU.subtract))
            prep_step(nc.vector.tensor_copy(rel_lo, part_i))
            assert done[0] == PARTS_MADE

            dve.wait_ge(weights_loaded, 16 * WEIGHTS)
            nc.vector.tensor_scalar(eps_col[:, :], eps_col[:, :], 1.0, None, ALU.add).then_inc(eps1_ready, 1)
            dve.wait_ge(x_loaded, 16 * len(node_cuts))

            def norm_x(m):
                for b in range(2):
                    q = 2 * m + b
                    for j in range(CHUNK):
                        nc.vector.bn_stats(stats[:, b, j, :], X[:, bass.ds((q * CHUNK + j) * D, D)]).then_inc(
                            ln_stats, 1)
                    dve.wait_ge(ln_stats, CHUNK * (q + 1))
                    dve.sem_inc(dve_turns, 1)
                    for j in range(CHUNK):
                        nc.vector.bn_aggr(mv[:, b, j, :], stats[:, b, j, :]).then_inc(ln_mv, 1)
                    dve.wait_ge(ln_std, q + 1)
                    if started(m):
                        dve.wait_ge(h_made, q - 1)
                    nc.vector.reciprocal(rstd[:, b, :], std[:, b, :]).then_inc(ln_rstd, 1)
                    dve.wait_ge(ln_rstd, q + 1)
                    nc.vector.scalar_tensor_tensor(out=nmr[:, b, :], in0=mv[:, b, :, 0], scalar=-1.0,
                                                   in1=rstd[:, b, :], op0=ALU.mult, op1=ALU.mult).then_inc(ln_nmr, 1)

            over_chunks(dve, norm_x)

            dve.wait_ge(flag_ready, 1)
            dve.wait_ge(col_ready, 3 * SUPERS)

            def messages(nw):
                def one_hot(c, n, i, step, w):
                    nc.vector.tensor_scalar(onehotT[0:WIN, c % 2, 0:n * TILES], dst_bc[c % 2][0:WIN, 0:n * TILES],
                                            win_node[0:WIN, bass.ds(w, 1)], None, ALU.is_equal).then_inc(
                                                onehotT_ready, 1)

                def merge_plan(c, n, i):
                    b = c % 2
                    dve.wait_ge(src_spread, i + 1)
                    if started(i - 1):
                        dve.wait_ge(merged, i - 1)
                    nc.vector.tensor_tensor(
                        same[0:n, b, :, 0:n],
                        src_bc[b][0:n, 0:n * TILES].rearrange("p (e t) -> p t e", t=TILES),
                        src_col[0:n, cols(i)].rearrange("p (t a) -> p t a", a=1).to_broadcast([n, TILES, n]),
                        ALU.is_equal).then_inc(same_ready, 1)
                    dve.wait_ge(same_ready, i + 1)
                    for t in range(TILES):
                        nc.vector.tensor_tensor_reduce(
                            out=masked[0:n, b, t, 0:n], in0=same[0:n, b, t, 0:n], in1=earlier[0:n, 0:n], scale=1.0,
                            scalar=0.0, op0=ALU.mult, op1=ALU.add,
                            accum_out=before[0:n, b, t:t + 1]).then_inc(before_ready, 1)
                    dve.wait_ge(before_ready, TILES * (i + 1))
                    nc.vector.tensor_scalar(dump_or_0[0:n, b, :], before[0:n, b, :], 1.0, dump_col[0:n, 0:1],
                                            ALU.min, ALU.mult).then_inc(dump_ready, 1)
                    dve.wait_ge(dump_ready, i + 1)
                    if started(i - 1):
                        dve.wait_ge(summed_ready, i - 1)
                    nc.vector.tensor_tensor(scatter_idx[0:n, c, :], dump_or_0[0:n, b, :], src_col[0:n, cols(i)],
                                            ALU.max).then_inc(scatter_idx_ready, 1)

                def add_h(c, n, k, i, step):
                    dve.wait_ge(ea_landed[c], 16 * (k + 1))
                    dve.wait_ge(h_gathered, step + 1)
                    if nw > 1 and started(step):
                        dve.wait_ge(h_added, step)
                    nc.vector.tensor_tensor(ea[0:n, c, :, :], ea[0:n, c, :, :], gath_ps[c % 2][0:n, :].rearrange(
                        "p (t d) -> p t d", t=TILES), ALU.add).then_inc(h_added, 1)

                def group(k, parts):
                    for c, n in enumerate(parts):
                        i = SUPERS * k + c
                        dve.wait_ge(dst_spread, i + 1)
                        if nw == 1:
                            one_hot(c, n, i, i, 0)
                            merge_plan(c, n, i)
                            add_h(c, n, k, i, i)
                        else:
                            merge_plan(c, n, i)
                            with dve.Fori(0, nw) as w:
                                one_hot(c, n, i, i * nw + w, w)
                                add_h(c, n, k, i, i * nw + w)

                over_groups(dve, group)

            both_ways(dve, messages)

            for t in range(TILES):
                dve.wait_ge(scattered[t], 16 * supers)

            def sum_accs(b, q, m):
                dve.wait_ge(accs_landed[b], 16 * TILES * (m + 1))
                nc.vector.tensor_tensor(accs[:, b, 0, :], accs[:, b, 0, :], accs[:, b, 1, :], ALU.add).then_inc(
                    half_summed, 1)
                dve.wait_ge(half_summed, q + 1)
                dve.wait_ge(pool_summed, q + 1)
                nc.vector.tensor_tensor(accs[:, b, 0, :], accs[:, b, 0, :], accs[:, b, 2, :], ALU.add).then_inc(
                    nodes_ready, 1)

            def first_product(b, q, j):
                n = CHUNK * q + j
                dve.wait_ge(h1_done, n + 1)
                nc.vector.tensor_tensor(h1[:, b, j, :], h1_ps[(CHUNK * b + j) % 2][:, 0:H], b1_bc[:, :],
                                        ALU.add).then_inc(h1_ready, 1)

            def first_stats(b, q, j):
                dve.wait_ge(h1_ready, CHUNK * q + j + 1)
                nc.vector.bn_stats(stats[:, b, j, :], h1[:, b, j, :]).then_inc(mlp_stats, 1)

            def first_moments(b, q):
                dve.wait_ge(mlp_stats, CHUNK * (q + 1))
                dve.sem_inc(dve_turns, 1)
                for j in range(CHUNK):
                    nc.vector.bn_aggr(mv[:, b, j, :], stats[:, b, j, :]).then_inc(mlp_mv, 1)

            def first_norm(b, q):
                dve.wait_ge(mlp_std, q + 1)
                nc.vector.reciprocal(rstd[:, b, :], std[:, b, :]).then_inc(mlp_rstd, 1)
                dve.wait_ge(mlp_rstd, q + 1)
                nc.vector.scalar_tensor_tensor(out=nmr[:, b, :], in0=mv[:, b, :, 0], scalar=-1.0,
                                               in1=rstd[:, b, :], op0=ALU.mult, op1=ALU.mult).then_inc(mlp_nmr, 1)

            def second_product(b, q, j):
                n = CHUNK * q + j
                own = X[:, bass.ds(n * D, D)]
                dve.wait_ge(b2_added, q + 1)
                dve.wait_ge(mlp_done, n + 1)
                nc.vector.tensor_tensor(own, own, mlp_ps[(CHUNK * b + j) % 2][:, 0:D], ALU.add).then_inc(x1_ready, 1)

            def second_stats(q, j):
                dve.wait_ge(x1_ready, CHUNK * q + j + 1)
                dve.sem_inc(dve_turns, 1)
                nc.vector.bn_stats(stats2[:, j, :], X[:, bass.ds((q * CHUNK + j) * D, D)]).then_inc(ln2_stats, 1)

            def second_moments(q):
                dve.wait_ge(ln2_stats, CHUNK * (q + 1))
                dve.sem_inc(dve_turns, 1)
                for j in range(CHUNK):
                    nc.vector.bn_aggr(mv2[:, j, :], stats2[:, j, :]).then_inc(ln2_mv, 1)

            def second_norm(q):
                dve.wait_ge(ln2_std, q + 1)
                if started(q):
                    dve.wait_ge(h2_ready, CHUNK * q)
                nc.vector.reciprocal(rstd2[:, :], std2[:, :]).then_inc(ln2_rstd, 1)
                dve.wait_ge(ln2_rstd, q + 1)
                nc.vector.scalar_tensor_tensor(out=nmr2[:, :], in0=mv2[:, :, 0], scalar=-1.0,
                                               in1=rstd2[:, :], op0=ALU.mult, op1=ALU.mult).then_inc(ln2_nmr, 1)

            def chunk(b, q, next_m, first=True, second=True):
                if first:
                    if started(q - 1):
                        dve.wait_ge(hn_turned, CHUNK * (q - 1))
                for j in range(CHUNK):
                    if first:
                        first_product(b, q, j)
                    if second:
                        second_product(1 - b, q - 1, j)
                    if first:
                        first_stats(b, q, j)
                    if second:
                        second_stats(q - 1, j)
                if first:
                    first_moments(b, q)
                if second:
                    second_moments(q - 1)
                if first:
                    first_norm(b, q)
                if next_m is not None:
                    sum_accs(1 - b, q + 1, next_m)
                if second:
                    second_norm(q - 1)

            sum_accs(0, 0, 0)
            chunk(0, 0, 0, second=False)
            chunk(1, 1, 1)
            if chunks > 4:
                with dve.Fori(1, chunks // 2 - 1) as m:
                    chunk(0, 2 * m, m)
                    chunk(1, 2 * m + 1, m + 1)
            chunk(0, chunks - 2, chunks // 2 - 1)
            chunk(1, chunks - 1, None)
            chunk(0, chunks, None, first=False)

            for b in range(2):
                dve.wait_ge(h2_stored[b], 16 * (chunks // 2))
            dve.wait_ge(agg_zeroed, 1)
            dve.wait_ge(deg_zeroed, 1)

            def one_hot(b, n, rel):
                nc.vector.tensor_tensor(
                    onehot[0:n, b, :, :],
                    lane[0:n, :].rearrange("p (a v) -> p a v", a=1).to_broadcast([n, TILES, WIN]),
                    rel.rearrange("p (t a) -> p t a", a=1).to_broadcast([n, TILES, WIN]),
                    ALU.is_equal).then_inc(onehot_ready, 1)

            def add_sums(b, step, base):
                at = bass.ds(base, WIN)
                dve.wait_ge(agg_done, step + 1)
                if started(step):
                    dve.wait_ge(sums_added, 2 * step)
                nc.vector.tensor_tensor(aggT[:, at], aggT[:, at], agg_ps[b][:, 0:WIN], ALU.add).then_inc(
                    sums_added, 1)
                nc.vector.tensor_tensor(deg[:, at], deg[:, at], deg_ps[b][0:1, 0:WIN], ALU.add).then_inc(
                    sums_added, 1)

            def sums(nw):
                def group(k, parts):
                    for c, n in enumerate(parts):
                        i = SUPERS * k + c
                        dve.wait_ge(gathered_landed[c], 16 * TILES * (k + 1))
                        nc.vector.tensor_tensor(
                            gathered[0:n, c, :, :], gathered[0:n, c, :, :],
                            w_col[0:n, cols(i)].rearrange("p (t a) -> p t a", a=1).to_broadcast([n, TILES, D]),
                            ALU.mult).then_inc(weighted, 1)
                        if nw == 1:
                            one_hot(c % 2, n, rel_col[0:n, cols(i)])
                            if started(i):
                                add_sums((c - 1) % 2, i - 1, dve.value_load(
                                    bases[0:1, bass.ds(i - 1, 1)], min_val=0, max_val=N - 1))
                        else:
                            with dve.Fori(0, nw) as w:
                                nc.vector.tensor_scalar(rel_win[0:n, :], rel_col[0:n, cols(i)],
                                                        win_first[0:n, bass.ds(w, 1)], None,
                                                        ALU.subtract).then_inc(rel_shifted, 1)
                                dve.wait_ge(rel_shifted, i * nw + w + 1)
                                one_hot(c % 2, n, rel_win[0:n, :])
                                add_sums(c % 2, i * nw + w, w * WIN)

                over_groups(dve, group)
                if nw == 1:
                    last = supers - 1
                    add_sums((len(tail) - 1) % 2, last, dve.value_load(
                        bases[0:1, last:last + 1], min_val=0, max_val=N - 1))
                dve.wait_ge(sums_added, 2 * supers * nw)

            both_ways(dve, sums)
            dve.sem_inc(agg_added, 1)

            dve.wait_ge(deg_loaded, 16)
            nc.vector.tensor_scalar(no_edge[:, :], deg_nodes[:, :], 0.0, None, ALU.is_equal).then_inc(no_edge_ready, 1)
            dve.wait_ge(no_edge_ready, 1)

            def results(m):
                for b in range(2):
                    q = 2 * m + b
                    dve.wait_ge(agg_turned, q + 1)
                    for j0, j1 in ((0, 4), (4, CHUNK)):
                        own = X[:, bass.ds((q * CHUNK + j0) * D, (j1 - j0) * D)]
                        nc.vector.tensor_tensor(own, own, bank[4 + 2 * b + j0 // 4][:, 0:(j1 - j0) * D],
                                                ALU.add).then_inc(agg_out, 1)
                for b in range(2):
                    q = 2 * m + b
                    own = X[:, bass.ds(q * CHUNK * D, CHUNK * D)]
                    dve.wait_ge(agg_out, 2 * (q + 1))
                    dve.wait_ge(own_ready, q + 1)
                    nc.vector.tensor_tensor(own, own, h2_in[:, b, :, :].rearrange("p j d -> p (j d)"),
                                            ALU.add).then_inc(result_ready, 1)

            over_chunks(dve, results)


_INS = ["x", "src", "dst", "edge_attr_128", "edge_weight", "L0_gnn_eps", "L0_gnn_W1", "L0_gnn_b1",
        "L0_gnn_gamma", "L0_gnn_beta", "L0_gnn_W2", "L0_gnn_b2"]


def kernel(**inputs):
    import numpy as _np
    import concourse.bacc as _bacc
    from concourse import mybir as _mybir
    from concourse.bass_utils import run_bass_kernel_spmd as _run

    nc = _bacc.Bacc("TRN2", target_bir_lowering=False, num_devices=1)
    arrays, args = {}, []
    for name in _INS:
        a = _np.ascontiguousarray(inputs[name])
        arrays[f"in_{name}"] = a
        args.append(nc.dram_tensor(f"in_{name}", a.shape, _mybir.dt.from_np(a.dtype), kind="ExternalInput").ap())
    shape = arrays["in_x"].shape
    args.append(nc.dram_tensor("out_0", shape, _mybir.dt.float32, kind="ExternalOutput").ap())
    build(nc, *args)
    r = _run(nc, [arrays], core_ids=[0])
    return r.results[0]["out_0"]
```

```python
from contextlib import ExitStack

import concourse.bass as bass
from concourse import mybir

P = 128
D = 128
H = 256
TILES = 4
SUPER = P * TILES
SUPERS = 4
GROUP = SUPER * SUPERS
WIN = 64
CHUNK = 7
TURN = -1
MOMENTS = 1
SECOND = CHUNK + 4
MOMENTS2 = SECOND + 1
H2 = MOMENTS2 + CHUNK
LN_EPS = 1e-5

ALU = mybir.AluOpType
ACT = mybir.ActivationFunctionType
AX_X = mybir.AxisListType.X
F32 = mybir.dt.float32
BF16 = mybir.dt.bfloat16
I32 = mybir.dt.int32


def build(nc, x, src, dst, edge_attr, edge_weight, eps, W1, b1, gamma, beta, W2, b2, out):
    N = x.shape[0]
    E = src.shape[0]
    NJ = -(-N // P)
    NP = NJ * P
    full_parts, rest_nodes = N // NJ, N % NJ
    DUMP = NP
    chunks = NJ // CHUNK
    assert full_parts >= 96 and full_parts < P
    assert NJ % (2 * CHUNK) == 0 and chunks >= 10
    windows = -(-N // WIN)
    G = E // GROUP
    rest = E % GROUP
    assert G >= 2 and rest % TILES == 0 and rest
    tail = [P] * (rest // SUPER) + ([rest % SUPER // TILES] if rest % SUPER else [])
    supers = SUPERS * G + len(tail)
    assert supers >= chunks
    ROWS = G + 1
    assert ROWS <= P
    widths = [P] * SUPERS

    def view_nodes(t):
        return t.rearrange("(p j) d -> p (j d)", j=NJ)

    def started(value):
        return not isinstance(value, int) or value > 0

    with ExitStack() as ctx:
        def dram(name, shape, dt):
            return nc.dram_tensor(name, shape, dt).ap()

        def sb(name, shape, dt=F32):
            return ctx.enter_context(nc.sbuf_tensor(name, shape, dt))

        def sem(name):
            return ctx.enter_context(nc.semaphore(name))

        h_dram = dram("h_scratch", [NP + WIN, D], F32)
        h2_dram = dram("h2_scratch", [NP, D], F32)
        acc_dram = [dram(f"acc_scratch{t}", [NP + P, D], F32) for t in range(TILES)]
        deg_dram = dram("deg_scratch", [NP], F32)

        X = sb("X", [P, NJ * D])
        src_col = sb("src_col", [P, ROWS * 16])
        rel_col = sb("rel_col", [P, ROWS * 16])
        w_col = sb("w_col", [P, ROWS * 16])
        bases = sb("bases", [1, ROWS * SUPERS], I32)
        ident = sb("ident", [P, P])
        ident_b = sb("ident_b", [P, P], BF16)
        earlier = sb("earlier", [P, P])
        lane = sb("lane", [P, WIN])
        win_node = sb("win_node", [P, windows])
        win_first = sb("win_first", [P, windows])
        dump_col = sb("dump_col", [P, 1])
        ones = sb("ones", [P, P])
        eps_col = sb("eps_col", [P, 1])
        ln_eps = sb("ln_eps", [P, 1])
        W1_sb = sb("W1_sb", [P, H])
        W2_sb = sb("W2_sb", [P, 2, D])
        b1_bc = sb("b1_bc", [P, H])
        b2_bc = sb("b2_bc", [P, D])
        gamma_col = sb("gamma_col", [P, 2])
        beta_col = sb("beta_col", [P, 2])
        flag_f = sb("flag_f", [1, 1])
        flag_i = sb("flag_i", [1, 1], I32)
        spread = sb("spread", [P, 4])
        mv = sb("mv", [P, 2, CHUNK, 2])
        stats = sb("stats", [P, 2, CHUNK, 6])
        std = sb("std", [P, 2, CHUNK])
        rstd = sb("rstd", [P, 2, CHUNK])
        nmr = sb("nmr", [P, 2, CHUNK])
        mv2 = sb("mv2", [P, CHUNK, 2])
        stats2 = sb("stats2", [P, CHUNK, 6])
        std2 = sb("std2", [P, CHUNK])
        rstd2 = sb("rstd2", [P, 2, CHUNK])
        nmr2 = sb("nmr2", [P, 2, CHUNK])
        deg_nodes = sb("deg_nodes", [P, NJ])

        aggT_words = NP + WIN
        nodes_words = CHUNK * (2 * TILES * D + 2 * D + 2 * H + 2 * D) + 2 * D + 4 * P
        arena_words = max(nodes_words, aggT_words + 2 * CHUNK * P) + max(aggT_words, 10240)
        arena = sb("arena", [P, arena_words])
        parts_at = arena_words - 2 * GROUP
        src_hi, src_lo, rel_hi, rel_lo = (
            arena[:, parts_at + n * GROUP // 2:parts_at + (n + 1) * GROUP // 2].bitcast(BF16) for n in range(4))
        place = [0]

        def area(words, restart=False):
            if restart:
                place[0] = 0
            a = arena[:, place[0]:place[0] + words]
            place[0] += words
            assert place[0] <= arena_words
            return a

        dst_i = area(GROUP, True).bitcast(I32)
        src_i = area(GROUP).bitcast(I32)
        w_rows = area(GROUP)
        dst_f = area(GROUP)
        src_f = area(GROUP)
        rel_f = area(GROUP)
        part_i = area(GROUP).bitcast(I32)
        h_out = area(2 * CHUNK * D).rearrange("p (b n) -> p b n", b=2)
        eh_out = area(2 * CHUNK * D).rearrange("p (b n) -> p b n", b=2)
        zeros = area(CHUNK * D)
        ea = area(SUPERS * TILES * D, True).rearrange("p (c t d) -> p c t d", c=SUPERS, t=TILES)
        hwin = area(SUPERS * D).rearrange("p (c d) -> p c d", c=SUPERS)
        onehotT = area(2 * SUPER).rearrange("p (b e) -> p b e", b=2)
        same = area(2 * TILES * P).rearrange("p (b t e) -> p b t e", b=2, t=TILES)
        masked = area(2 * TILES * P).rearrange("p (b t e) -> p b t e", b=2, t=TILES)
        summed = area(2 * TILES * D).rearrange("p (b t d) -> p b t d", b=2, t=TILES)
        before = area(2 * TILES).rearrange("p (b t) -> p b t", b=2)
        dump_or_0 = area(2 * TILES).rearrange("p (b t) -> p b t", b=2)
        scatter_idx = area(SUPERS * TILES).bitcast(I32).rearrange("p (c t) -> p c t", c=SUPERS)
        accs = area(2 * TILES * CHUNK * D, True).rearrange("p (b r n) -> p b r n", b=2, r=TILES)
        nodes = area(2 * CHUNK * D).rearrange("p (b n) -> p b n", b=2)
        nodesT = area(2 * D).rearrange("p (b d) -> p b d", b=2)
        h1 = area(2 * CHUNK * H).rearrange("p (b j f) -> p b j f", b=2, j=CHUNK)
        reluT = area(2 * 2 * P).rearrange("p (b s n) -> p b s n", b=2, s=2)
        h2_out = area(2 * CHUNK * D).rearrange("p (b n) -> p b n", b=2)
        assert place[0] == nodes_words
        deg = area(aggT_words, True)[0:1, :]
        aggT = arena[:, arena_words - aggT_words:]
        gathered = sb("gathered", [P, SUPERS, TILES, D])
        gather_idx = sb("gather_idx", [P, SUPERS, TILES], I32)
        rel_win = sb("rel_win", [P, TILES])
        onehot = sb("onehot", [P, 2, TILES, WIN])
        aggT_chunk = arena[:, aggT_words:aggT_words + 2 * CHUNK * P].rearrange("p (b j n) -> p b j n", b=2, j=CHUNK)
        h2_in = area(NJ * D, True)
        no_edge = sb("no_edge", [P, NJ])
        base_col = sb("base_col", [P, SUPERS])

        bank = [ctx.enter_context(nc.psum_tensor(f"bank{b}", [P, 512], F32)) for b in range(8)]
        dst_bc, src_bc, gath_ps, sum_ps = bank[0:2], bank[2:4], bank[4:6], bank[6:8]
        nodesT_ps, h1_ps, hnT_ps, mlp_ps = bank[0:2], bank[2:4], bank[4:6], bank[6:8]
        agg_ps, deg_ps = bank[0:2], bank[2:4]

        idx_loaded = sem("idx_loaded")
        idx_zeroed = sem("idx_zeroed")
        const_ready = sem("const_ready")
        weights_loaded = sem("weights_loaded")
        x_zeroed = sem("x_zeroed")
        x_loaded = sem("x_loaded")
        prep = sem("prep")
        REL_MADE, WAY_OUT_MADE, FLAG_MADE, ROWS_MADE, PARTS_MADE = 2, 6, 8, 12, 19
        way_out_turned = sem("way_out_turned")
        flag_spread = sem("flag_spread")
        h_made = sem("h_made")
        eps1_ready = sem("eps1_ready")
        eh_ready = sem("eh_ready")
        sums_added = sem("sums_added")
        pool_turns = sem("pool_turns")
        dve_turns = sem("dve_turns")
        rel_cut = sem("rel_cut")
        flag_ready = sem("flag_ready")
        col_turned = sem("col_turned")
        col_ready = sem("col_ready")
        zeros_ready = sem("zeros_ready")
        cleared = sem("cleared")
        ln_stats = sem("ln_stats")
        ln_mv = sem("ln_mv")
        ln_std = sem("ln_std")
        ln_rstd = sem("ln_rstd")
        ln_nmr = sem("ln_nmr")
        h_stored = [sem(f"h_stored{b}") for b in range(2)]
        eh_stored = [sem(f"eh_stored{b}") for b in range(2)]
        ea_landed = [sem(f"ea_landed{c}") for c in range(SUPERS)]
        hwin_landed = [sem(f"hwin_landed{c}") for c in range(SUPERS)]
        dst_spread = sem("dst_spread")
        src_spread = sem("src_spread")
        onehotT_ready = sem("onehotT_ready")
        h_gathered = sem("h_gathered")
        h_added = sem("h_added")
        message_ready = sem("message_ready")
        same_ready = sem("same_ready")
        before_ready = sem("before_ready")
        dump_ready = sem("dump_ready")
        scatter_idx_ready = sem("scatter_idx_ready")
        merged = sem("merged")
        summed_ready = sem("summed_ready")
        scattered = [sem(f"scattered{t}") for t in range(TILES)]
        accs_landed = [sem(f"accs_landed{b}") for b in range(2)]
        pair_summed = sem("pair_summed")
        first_summed = sem("first_summed")
        nodes_ready = sem("nodes_ready")
        nodes_turned = sem("nodes_turned")
        nodesT_ready = sem("nodesT_ready")
        h1_done = sem("h1_done")
        h1_ready = sem("h1_ready")
        mlp_stats = sem("mlp_stats")
        mlp_mv = sem("mlp_mv")
        mlp_std = sem("mlp_std")
        mlp_rstd = sem("mlp_rstd")
        mlp_nmr = sem("mlp_nmr")
        hn_ready = sem("hn_ready")
        hn_turned = sem("hn_turned")
        reluT_ready = sem("reluT_ready")
        mlp_done = sem("mlp_done")
        b2_added = sem("b2_added")
        x1_ready = sem("x1_ready")
        ln2_stats = sem("ln2_stats")
        ln2_mv = sem("ln2_mv")
        ln2_std = sem("ln2_std")
        ln2_rstd = sem("ln2_rstd")
        ln2_nmr = sem("ln2_nmr")
        h2_ready = sem("h2_ready")
        h2_stored = [sem(f"h2_stored{b}") for b in range(2)]
        agg_zeroed = sem("agg_zeroed")
        deg_zeroed = sem("deg_zeroed")
        gather_idx_ready = sem("gather_idx_ready")
        gathered_landed = [sem(f"gathered_landed{c}") for c in range(SUPERS)]
        weighted = sem("weighted")
        rel_shifted = sem("rel_shifted")
        onehot_ready = sem("onehot_ready")
        agg_done = sem("agg_done")
        agg_added = sem("agg_added")
        deg_stored = sem("deg_stored")
        deg_loaded = sem("deg_loaded")
        no_edge_ready = sem("no_edge_ready")
        h2_loaded = sem("h2_loaded")
        first_h2_loaded = sem("first_h2_loaded")
        agg_copied = sem("agg_copied")
        agg_turned = sem("agg_turned")
        agg_out = sem("agg_out")
        own_ready = sem("own_ready")
        result_ready = sem("result_ready")
        stored = sem("stored")

        CONSTS = 11
        FIRST_CLEARED, LAST_CLEARED = 4, 6
        H2_CUTS = ((1, 16), (16, P))
        CLEARS = TILES + 4 + (TILES - 2) * chunks - LAST_CLEARED
        WEIGHTS = 7

        def part_cuts(n):
            cut = n // 16 * 16
            return [(a, b) for a, b in ((0, cut), (cut, n)) if b > a]

        node_cuts = [(a, b, NJ) for a, b in part_cuts(full_parts)]
        if rest_nodes:
            node_cuts.append((full_parts, full_parts + 1, rest_nodes))
        row_cuts = [(a, b, GROUP) for a, b in part_cuts(G)] + [(G, G + 1, rest)]

        def both_ways(eng, program):
            fast = eng.value_load(flag_i[0:1, 0:1], min_val=0, max_val=1)
            with eng.If(fast):
                program(1)
            with eng.Else():
                program(windows)

        def over_groups(eng, group):
            group(0, widths)
            with eng.Fori(1, G) as k:
                group(k, widths)
            group(G, tail)

        def over_chunks(eng, pair):
            pair(0)
            if chunks > 2:
                with eng.Fori(1, chunks // 2) as m:
                    pair(m)

        def over_turns(turn):
            first_pairs = -(-H2 // (2 * CHUNK))

            def run(eng):
                def chunk(m, b):
                    for t in range(CHUNK):
                        turn(m, b, t)

                for q in range(2 * first_pairs):
                    chunk(q // 2, q % 2)
                with eng.Fori(first_pairs, chunks // 2 - 1) as m:
                    chunk(m, 0)
                    chunk(m, 1)
                for q in range(chunks - 2, chunks + -(-H2 // CHUNK)):
                    chunk(q // 2, q % 2)
            return run

        def lagging(turn, lag):
            m, b, t = turn
            chunk, j = divmod(t - lag, CHUNK)
            pair, b = divmod(b + chunk, 2)
            if isinstance(m, int) and not 0 <= 2 * (m + pair) + b < chunks:
                return []
            return [(m + pair, b, j)]

        def number(m, b, j=0):
            return CHUNK * (2 * m + b) + j, (CHUNK * b + j) % 2

        def over_windows(eng, nw, step):
            if nw == 1:
                step(0)
            else:
                with eng.Fori(0, nw) as w:
                    step(w)

        def cols(i):
            return bass.ds(TILES * i, TILES)

        block = ctx.enter_context(nc.Block())

        @block.sync
        def _(sp):
            def clear_chunks(t, q0, q1):
                n = q1 - q0
                sp.dma_start(
                    view_nodes(acc_dram[t][0:NP, :])[:, q0 * CHUNK * D:q1 * CHUNK * D].rearrange(
                        "p (q n) -> p q n", q=n),
                    zeros[:, :].rearrange("p (a n) -> p a n", a=1).to_broadcast([P, n, CHUNK * D]),
                ).then_inc(cleared, 16)

            sp.wait_ge(zeros_ready, 1)
            clear_chunks(1, 0, FIRST_CLEARED)
            sp.wait_ge(idx_zeroed, 3)
            for rows, of in ((dst_i, dst), (src_i, src), (w_rows, edge_weight)):
                for a, b, n in row_cuts:
                    sp.dma_start(rows[a:b, 0:n], of[a * GROUP:a * GROUP + (b - a) * n].rearrange(
                        "(k e) -> k e", e=n)).then_inc(idx_loaded, 16)
            with nc.allow_non_contiguous_dma(reason="one dst of each supertile, once"):
                nb = -(-E // SUPER)
                sp.dma_start(bases[0:1, 0:nb - 1], dst[0:(nb - 1) * SUPER].rearrange(
                    "(a s e) -> a s e", a=1, e=SUPER)[:, :, 0]).then_inc(idx_loaded, 16)
                sp.dma_start(bases[0:1, nb - 1:nb], dst[(nb - 1) * SUPER:(nb - 1) * SUPER + 1].rearrange(
                    "(a s) -> a s", a=1)).then_inc(idx_loaded, 16)
                sp.dma_start(gamma_col[:, :], gamma.rearrange("(s p) -> p s", p=P)).then_inc(weights_loaded, 16)
                sp.dma_start(beta_col[:, :], beta.rearrange("(s p) -> p s", p=P)).then_inc(weights_loaded, 16)
            sp.wait_ge(x_zeroed, 1)
            for a, b, n in node_cuts:
                sp.dma_start(X[a:b, 0:n * D], x[a * NJ:a * NJ + (b - a) * n, :].rearrange(
                    "(p j) d -> p (j d)", j=n)).then_inc(x_loaded, 16)
            sp.dma_start(W1_sb[:, :], W1).then_inc(weights_loaded, 16)
            sp.dma_start(W2_sb[:, :, :], W2.rearrange("(s p) d -> p s d", p=P)).then_inc(weights_loaded, 16)
            for row, of in ((b1_bc, b1), (b2_bc, b2), (eps_col, eps)):
                sp.dma_start(row[:, :], of.rearrange("(a n) -> a n", a=1).to_broadcast(row.shape)).then_inc(
                    weights_loaded, 16)

            for t in range(TILES):
                sp.dma_start(acc_dram[t][DUMP:DUMP + P, :], zeros[:, 0:D]).then_inc(cleared, 16)
            sp.dma_start(h_dram[NP:NP + WIN, :], zeros[0:WIN, 0:D]).then_inc(cleared, 16)
            clear_chunks(1, FIRST_CLEARED, chunks)

            def store_h(m, both=True):
                for b in range(2):
                    q = 2 * m + b
                    at = bass.ds(q * CHUNK * D, CHUNK * D)
                    for t in (2, 3) if both else (2,):
                        sp.dma_start(view_nodes(acc_dram[t][0:NP, :])[:, at], zeros).then_inc(cleared, 16)
                    sp.wait_ge(h_made, q + 1)
                    sp.dma_start(view_nodes(h_dram[0:NP, :])[:, at], h_out[:, b, :]).then_inc(h_stored[b], 16)
                    sp.wait_ge(eh_ready, q + 1)
                    sp.dma_start(view_nodes(acc_dram[0][0:NP, :])[:, at], eh_out[:, b, :]).then_inc(
                        eh_stored[b], 16)

            store_h(0)
            last_both = (chunks - LAST_CLEARED) // 2
            with sp.Fori(1, last_both) as m:
                store_h(m)
            with sp.Fori(last_both, chunks // 2) as m:
                store_h(m, both=False)

            sp.wait_ge(prep, PARTS_MADE)
            sp.wait_ge(col_ready, 3 * SUPERS)

            def load_ea(c, n, k, i):
                if started(k):
                    sp.wait_ge(merged, i - SUPERS + 1)
                sp.dma_start(ea[0:n, c, :, :], edge_attr[bass.ds(SUPER * i, n * TILES), :].rearrange(
                    "(p t) d -> p t d", t=TILES)).then_inc(ea_landed[c], 16)

            for c in range(SUPERS):
                load_ea(c, P, 0, c)

            for b in range(2):
                sp.wait_ge(h_stored[b], 16 * (chunks // 2))
            sp.wait_ge(cleared, 16 * (CLEARS - 1))
            sp.wait_ge(flag_ready, 1)

            def loads(nw):
                def group(k, parts):
                    for c, n in enumerate(parts):
                        i = SUPERS * k + c
                        if started(k):
                            load_ea(c, n, k, i)

                        def window(w):
                            step = i * nw + w
                            last = i - SUPERS + 1 if nw == 1 else step
                            if started(last):
                                sp.wait_ge(h_gathered, last)
                            if nw == 1:
                                base = sp.value_load(bases[0:1, bass.ds(i, 1)], min_val=0, max_val=N - 1)
                            else:
                                base = w * WIN
                            sp.dma_start(hwin[0:WIN, c, :], h_dram[bass.ds(base, WIN), :]).then_inc(
                                hwin_landed[c], 16)

                        over_windows(sp, nw, window)
                    if not started(k):
                        clear_chunks(3, chunks - LAST_CLEARED, chunks)

                over_groups(sp, group)

            both_ways(sp, loads)

            for t in range(TILES):
                sp.wait_ge(scattered[t], 16 * supers)

            def load_accs(m, b):
                q = 2 * m + b
                if started(q - 1):
                    sp.wait_ge(nodes_ready, q - 1)
                for t in range(TILES):
                    sp.dma_start(accs[:, b, t, :], view_nodes(acc_dram[t][0:NP, :])[
                        :, bass.ds(q * CHUNK * D, CHUNK * D)]).then_inc(accs_landed[b], 16)

            def store_h2(m, b):
                q = 2 * m + b
                sp.wait_ge(h2_ready, CHUNK * (q + 1))
                sp.dma_start(view_nodes(h2_dram)[:, bass.ds(q * CHUNK * D, CHUNK * D)], h2_out[:, b, :]).then_inc(
                    h2_stored[b], 16)

            for q in range(6):
                load_accs(q // 2, q % 2)
            with sp.Fori(3, chunks // 2) as m:
                for b in range(2):
                    store_h2(m - 3, b)
                    load_accs(m, b)
            for q in range(chunks - 6, chunks):
                store_h2(q // 2, q % 2)

            for b in range(2):
                sp.wait_ge(h2_stored[b], 16 * (chunks // 2))
            with sp.Fori(0, chunks) as q:
                sp.wait_ge(agg_done, q + 1)
                at = bass.ds(q * CHUNK * D, CHUNK * D)
                for a, b in H2_CUTS:
                    sp.dma_start(h2_in[a:b, at], view_nodes(h2_dram)[a:b, at]).then_inc(h2_loaded, 16)

            sp.wait_ge(agg_added, 1)
            sp.dma_start(deg_dram.rearrange("(a n) -> a n", a=1), deg[:, 0:NP]).then_inc(deg_stored, 16)
            sp.wait_ge(deg_stored, 16)
            sp.dma_start(deg_nodes[:, :], deg_dram.rearrange("(p j) -> p j", j=NJ)).then_inc(deg_loaded, 16)
            sp.dma_start(h2_in[0:1, :], view_nodes(h2_dram)[0:1, :]).then_inc(first_h2_loaded, 16)

            def store_result(m):
                sp.wait_ge(result_ready, 2 * (m + 1))
                at = bass.ds(m * 2 * CHUNK * D, 2 * CHUNK * D)
                for a, b in part_cuts(full_parts):
                    sp.dma_start(out[a * NJ:b * NJ, :].rearrange("(p j) d -> p (j d)", j=NJ)[:, at],
                                 X[a:b, at]).then_inc(stored, 16)

            with sp.Fori(0, chunks // 2) as m:
                store_result(m)
            if rest_nodes:
                sp.dma_start(out[full_parts * NJ:N, :].rearrange("(p j) d -> p (j d)", p=1),
                             X[full_parts:full_parts + 1, 0:rest_nodes * D]).then_inc(stored, 16)
            sp.wait_ge(stored, 16 * (len(part_cuts(full_parts)) * chunks // 2 + (rest_nodes > 0)))


        @block.gpsimd
        def _(pool):
            nc.gpsimd.memset(zeros, 0.0).then_inc(zeros_ready, 1)
            for rows in (dst_i, src_i, w_rows):
                nc.gpsimd.memset(rows, 0).then_inc(idx_zeroed, 1)
            nc.gpsimd.memset(ident[:, :], 0.0).then_inc(const_ready, 1)
            nc.gpsimd.memset(earlier[:, :], 1.0).then_inc(const_ready, 1)
            nc.gpsimd.memset(ones[:, :], 1.0).then_inc(const_ready, 1)
            nc.gpsimd.memset(ln_eps[:, :], LN_EPS).then_inc(const_ready, 1)
            nc.gpsimd.iota(lane[:, :], pattern=[[1, WIN]], base=0, channel_multiplier=0,
                           allow_small_or_imprecise_dtypes=True).then_inc(const_ready, 1)
            nc.gpsimd.iota(win_node[:, :], pattern=[[WIN, windows]], base=0, channel_multiplier=1,
                           allow_small_or_imprecise_dtypes=True).then_inc(const_ready, 1)
            nc.gpsimd.iota(win_first[:, :], pattern=[[WIN, windows]], base=0, channel_multiplier=0,
                           allow_small_or_imprecise_dtypes=True).then_inc(const_ready, 1)
            nc.gpsimd.iota(dump_col[:, :], pattern=[[0, 1]], base=DUMP, channel_multiplier=1,
                           allow_small_or_imprecise_dtypes=True).then_inc(const_ready, 1)
            pool.wait_ge(const_ready, 8)
            nc.gpsimd.affine_select(out=ident[:, :], in_=ident[:, :], compare_op=ALU.not_equal, fill=1.0,
                                    base=0, pattern=[[-1, P]], channel_multiplier=1).then_inc(const_ready, 1)
            nc.gpsimd.affine_select(out=earlier[:, :], in_=earlier[:, :], compare_op=ALU.is_ge, fill=0.0,
                                    base=-1, pattern=[[-1, P]], channel_multiplier=1).then_inc(const_ready, 1)
            pool.wait_ge(const_ready, 10)
            nc.gpsimd.tensor_copy(ident_b[:, :], ident[:, :]).then_inc(const_ready, 1)
            pool.wait_ge(prep, REL_MADE)
            nc.gpsimd.affine_select(out=rel_f, in_=rel_f, compare_op=ALU.is_ge, fill=0.0, base=E - 1,
                                    pattern=[[-1, GROUP]], channel_multiplier=-GROUP).then_inc(rel_cut, 1)

            pool.wait_ge(weights_loaded, 16 * WEIGHTS)

            def add_b2(m):
                for b in range(2):
                    q = 2 * m + b
                    pool.wait_ge(h_made, q + 1)
                    at = bass.ds(q * CHUNK * D, CHUNK * D)
                    nc.gpsimd.tensor_tensor(
                        X[:, at].rearrange("p (j d) -> p j d", d=D), X[:, at].rearrange("p (j d) -> p j d", d=D),
                        b2_bc[:, :].rearrange("p (a d) -> p a d", a=1).to_broadcast([P, CHUNK, D]),
                        ALU.add).then_inc(b2_added, 1)

            over_chunks(pool, add_b2)

            pool.wait_ge(cleared, 16 * CLEARS)
            for b in range(2):
                pool.wait_ge(eh_stored[b], 16 * (chunks // 2))

            def scatter(k, parts):
                for c, n in enumerate(parts):
                    i = SUPERS * k + c
                    pool.wait_ge(scatter_idx_ready, i + 1)
                    pool.wait_ge(summed_ready, i + 1)
                    for t in range(TILES):
                        if started(i):
                            pool.wait_ge(scattered[t], 16 * i)
                        pool.sem_inc(pool_turns, 1)
                        nc.gpsimd.indirect_dma_start(
                            acc_dram[t], bass.IndirectOffsetOnAxis(scatter_idx[0:n, c, t:t + 1], 0),
                            summed[0:n, c % 2, t, :], None, compute_op=ALU.add).then_inc(scattered[t], 16)

            over_groups(pool, scatter)

            def sum_all(m, b):
                q = 2 * m + b
                pool.wait_ge(accs_landed[b], 16 * TILES * (m + 1))
                for t in (0, 2):
                    nc.gpsimd.tensor_tensor(accs[:, b, t, :], accs[:, b, t, :], accs[:, b, t + 1, :],
                                            ALU.add).then_inc(pair_summed, 1)
                pool.wait_ge(pair_summed, 2 * q)
                if started(q - 1):
                    pool.wait_ge(nodes_turned, number(m, b)[0] - CHUNK)
                nc.gpsimd.tensor_tensor(nodes[:, b, :], accs[:, b, 0, :], accs[:, b, 2, :], ALU.add).then_inc(
                    nodes_ready, 1)

            def norm(m, b):
                pool.wait_ge(mlp_nmr, 2 * m + b + 1)
                pool.sem_inc(pool_turns, 1)
                for j in range(CHUNK):
                    nc.gpsimd.tensor_scalar(h1[:, b, j, :], h1[:, b, j, :], rstd[:, b, j:j + 1],
                                            nmr[:, b, j:j + 1], ALU.mult, ALU.add).then_inc(hn_ready, 1)

            pool.wait_ge(nodes_ready, 1)
            sum_all(0, 1)
            sum_all(1, 0)
            with pool.Fori(0, chunks // 2 - 2) as m:
                norm(m, 0)
                sum_all(m + 1, 1)
                norm(m, 1)
                sum_all(m + 2, 0)
            norm(chunks // 2 - 2, 0)
            sum_all(chunks // 2 - 1, 1)
            norm(chunks // 2 - 2, 1)
            for b in range(2):
                norm(chunks // 2 - 1, b)

            for b in range(2):
                pool.wait_ge(h2_stored[b], 16 * (chunks // 2))

            def gathers(nw):
                def group(k, parts):
                    for c, n in enumerate(parts):
                        i = SUPERS * k + c
                        pool.wait_ge(gather_idx_ready, i + 1)
                        if started(i - SUPERS + 1):
                            pool.wait_ge(agg_done, (i - SUPERS + 1) * nw)
                        pool.sem_inc(pool_turns, 1)
                        for t in range(TILES):
                            nc.gpsimd.indirect_dma_start(
                                gathered[0:n, c, t, :], None, h2_dram,
                                bass.IndirectOffsetOnAxis(gather_idx[0:n, c, t:t + 1], 0)).then_inc(gathered_landed[c], 16)

                over_groups(pool, group)

            both_ways(pool, gathers)

            pool.wait_ge(h2_loaded, 16 * len(H2_CUTS) * chunks)
            pool.wait_ge(first_h2_loaded, 16)
            pool.wait_ge(no_edge_ready, 1)
            with pool.Fori(0, chunks) as q:
                own = h2_in[:, bass.ds(q * CHUNK * D, CHUNK * D)].rearrange("p (j d) -> p j d", d=D)
                nc.gpsimd.tensor_tensor(
                    own, own, no_edge[:, bass.ds(q * CHUNK, CHUNK)].rearrange("p (j a) -> p j a", a=1).to_broadcast(
                        [P, CHUNK, D]), ALU.mult).then_inc(own_ready, 1)

        @block.tensor
        def _(pe):
            pe.wait_ge(const_ready, CONSTS)
            pe.wait_ge(prep, WAY_OUT_MADE)
            nc.tensor.transpose(bank[0][0:1, 0:P], spread[:, 3:4], ident[:, :]).then_inc(way_out_turned, 1)
            pe.wait_ge(prep, FLAG_MADE)
            nc.tensor.matmul(bank[1][:, 0:1], ones[0:1, :], flag_f[:, :], start=True, stop=True).then_inc(
                flag_spread, 1)
            pe.wait_ge(prep, ROWS_MADE)
            n = 0
            for rows in (src_f, rel_f, w_rows):
                for c in range(SUPERS):
                    if n >= 2:
                        pe.wait_ge(col_ready, n - 1)
                    for t in range(TILES):
                        last = nc.tensor.transpose(bank[2 + n % 2][:, t * P:(t + 1) * P],
                                                   rows[:, c * SUPER + t:(c + 1) * SUPER:TILES], ident[:, :])
                    last.then_inc(col_turned, 1)
                    n += 1

            pe.wait_ge(flag_ready, 1)
            pe.wait_ge(prep, PARTS_MADE)
            pe.wait_ge(col_ready, 3 * SUPERS)

            def edges(nw):
                def spread_rows(k, c, i):
                    b = c % 2
                    pick = ident_b[:, bass.ds(k, 1)].to_broadcast([P, P])
                    e = slice(c * SUPER, (c + 1) * SUPER)
                    if started((i - 1) * nw):
                        pe.wait_ge(onehotT_ready, (i - 1) * nw)
                    nc.tensor.matmul(dst_bc[b][:, :], pick, rel_hi[:, e], start=True, stop=False)
                    nc.tensor.matmul(dst_bc[b][:, :], pick, rel_lo[:, e], start=False, stop=True).then_inc(
                        dst_spread, 1)
                    if started(i - 1):
                        pe.wait_ge(same_ready, i - 1)
                    nc.tensor.matmul(src_bc[b][:, :], pick, src_hi[:, e], start=True, stop=False)
                    nc.tensor.matmul(src_bc[b][:, :], pick, src_lo[:, e], start=False, stop=True).then_inc(
                        src_spread, 1)

                def gather(k, c, n, i):
                    b = c % 2

                    def window(w):
                        step = i * nw + w
                        pe.wait_ge(onehotT_ready, step + 1)
                        pe.wait_ge(hwin_landed[c], 16 * (k * nw + w + 1))
                        last = i - 1 if nw == 1 else step
                        if started(last):
                            pe.wait_ge(h_added, last)
                        for t in range(TILES):
                            mm = nc.tensor.matmul(gath_ps[b][0:n, t * D:(t + 1) * D],
                                                  onehotT[0:WIN, b, t:n * TILES:TILES], hwin[0:WIN, c, :],
                                                  start=True, stop=True)
                        mm.then_inc(h_gathered, 1)

                    over_windows(pe, nw, window)

                def merge(c, n, i):
                    b = c % 2
                    pe.wait_ge(same_ready, i + 1)
                    pe.wait_ge(message_ready, i + 1)
                    if started(i - 1):
                        pe.wait_ge(summed_ready, i - 1)
                    for t in range(TILES):
                        mm = nc.tensor.matmul(sum_ps[b][0:n, t * D:(t + 1) * D], same[0:n, b, t, 0:n],
                                              ea[0:n, c, t, :], start=True, stop=True)
                    mm.then_inc(merged, 1)

                def group(k, parts, following):
                    for c, n in enumerate(parts):
                        i = SUPERS * k + c
                        ahead = (k, c + 1, parts[c + 1]) if c + 1 < len(parts) else following
                        if ahead:
                            spread_rows(ahead[0], ahead[1], i + 1)
                        merge(c, n, i)
                        if ahead:
                            gather(*ahead, i + 1)

                spread_rows(0, 0, 0)
                gather(0, 0, P, 0)
                group(0, widths, (1, 0, P))
                with pe.Fori(1, G) as k:
                    group(k, widths, (k + 1, 0, P))
                group(G, tail, None)

            both_ways(pe, edges)

            for t in range(TILES):
                pe.wait_ge(scattered[t], 16 * supers)
            pe.wait_ge(weights_loaded, 16 * WEIGHTS)

            def turn_nodes(m, b, j):
                n, s = number(m, b, j)
                if j == 0:
                    pe.wait_ge(nodes_ready, 2 * m + b + 1)
                if started(n - 1):
                    pe.wait_ge(nodesT_ready, n - 1)
                nc.tensor.transpose(nodesT_ps[s][:, 0:P], nodes[:, b, j * D:(j + 1) * D],
                                    ident[:, :]).then_inc(nodes_turned, 1)

            def first_product(m, b, j):
                n, s = number(m, b, j)
                pe.wait_ge(nodesT_ready, n + 1)
                if started(n - 1):
                    pe.wait_ge(h1_ready, n - 1)
                nc.tensor.matmul(h1_ps[s][:, 0:H], nodesT[:, s, :], W1_sb[:, :], start=True,
                                 stop=True).then_inc(h1_done, 1)

            def turn_hn(m, b, j):
                n, s = number(m, b, j)
                pe.wait_ge(hn_ready, n + 1)
                if started(n - 1):
                    pe.wait_ge(reluT_ready, 2 * (n - 1))
                for half in range(2):
                    turn = nc.tensor.transpose(hnT_ps[s][:, half * P:(half + 1) * P],
                                               h1[:, b, j, half * P:(half + 1) * P], ident[:, :])
                turn.then_inc(hn_turned, 1)

            def second_product(m, b, j):
                n, s = number(m, b, j)
                pe.wait_ge(reluT_ready, 2 * (n + 1))
                if started(n - 1):
                    pe.wait_ge(x1_ready, n - 1)
                for half in range(2):
                    mm = nc.tensor.matmul(mlp_ps[s][:, 0:D], reluT[:, s, half, :], W2_sb[:, half, :],
                                          start=half == 0, stop=half == 1)
                mm.then_inc(mlp_done, 1)

            def turn(*at):
                for node in lagging(at, TURN):
                    turn_nodes(*node)
                for node in lagging(at, SECOND - 1):
                    turn_hn(*node)
                for node in lagging(at, 0):
                    first_product(*node)
                for node in lagging(at, SECOND):
                    second_product(*node)

            turn_nodes(0, 0, 0)
            over_turns(turn)(pe)

            def sums(nw):
                def group(k, parts):
                    for c, n in enumerate(parts):
                        i = SUPERS * k + c
                        b = c % 2

                        def window(w):
                            step = i * nw + w
                            pe.wait_ge(weighted, TILES * (i + 1))
                            pe.wait_ge(onehot_ready, step + 1)
                            last = step - 1 if nw == 1 else step
                            if started(last):
                                pe.wait_ge(sums_added, 2 * last)
                            for t in range(TILES):
                                nc.tensor.matmul(agg_ps[b][:, 0:WIN], gathered[0:n, c, t, :], onehot[0:n, b, t, :],
                                                 start=t == 0, stop=t == TILES - 1)
                            for t in range(TILES):
                                mm = nc.tensor.matmul(deg_ps[b][0:1, 0:WIN], ones[0:n, 0:1], onehot[0:n, b, t, :],
                                                      start=t == 0, stop=t == TILES - 1)
                            mm.then_inc(agg_done, 1)

                        over_windows(pe, nw, window)

                over_groups(pe, group)

            both_ways(pe, sums)

            pe.wait_ge(agg_added, 1)

            def turns(m):
                for b in range(2):
                    q = 2 * m + b
                    pe.wait_ge(agg_copied, q + 1)
                    if started(q - 1):
                        pe.wait_ge(agg_out, 2 * (q - 1))
                    for j in range(CHUNK):
                        turn = nc.tensor.transpose(bank[4 + 2 * b + j // 4][:, j % 4 * D:j % 4 * D + D],
                                                   aggT_chunk[:, b, j, :], ident[:, :])
                    turn.then_inc(agg_turned, 1)

            over_chunks(pe, turns)

        @block.scalar
        def _(act):
            n = 0
            for col in (src_col, rel_col, w_col):
                for c in range(SUPERS):
                    act.wait_ge(col_turned, n + 1)
                    nc.scalar.copy(
                        col[:, :].rearrange("p (k c t) -> p c t k", c=SUPERS, t=TILES)[:, c, :, :],
                        bank[2 + n % 2][:, :].rearrange("p (t k) -> p t k", t=TILES)[:, :, 0:ROWS],
                    ).then_inc(col_ready, 1)
                    n += 1

            act.wait_ge(const_ready, CONSTS)
            act.wait_ge(weights_loaded, 16 * WEIGHTS)

            def norm_x(m):
                for b in range(2):
                    q = 2 * m + b
                    act.wait_ge(ln_mv, CHUNK * (q + 1))
                    nc.scalar.activation(std[:, b, :], mv[:, b, :, 1], ACT.Sqrt, bias=ln_eps[:, 0:1]).then_inc(
                        ln_std, 1)
                    act.wait_ge(ln_nmr, q + 1)
                    if started(m):
                        act.wait_ge(h_stored[b], 16 * m)
                        act.wait_ge(eh_ready, q - 1)
                    for j in range(CHUNK):
                        last = nc.scalar.activation(h_out[:, b, j * D:(j + 1) * D],
                                                    X[:, bass.ds((q * CHUNK + j) * D, D)], ACT.Relu,
                                                    scale=rstd[:, b, j:j + 1], bias=nmr[:, b, j:j + 1])
                    last.then_inc(h_made, 1)

            over_chunks(act, norm_x)

            act.wait_ge(flag_ready, 1)
            for b in range(2):
                act.wait_ge(h_stored[b], 16 * (chunks // 2))

            def messages(nw):
                def group(k, parts):
                    for c, n in enumerate(parts):
                        i = SUPERS * k + c
                        b = c % 2
                        act.wait_ge(h_added, (i + 1) * nw)
                        nc.scalar.activation(ea[0:n, c, :, :], ea[0:n, c, :, :], ACT.Relu).then_inc(message_ready, 1)
                        act.wait_ge(merged, i + 1)
                        if started(i - 1):
                            for t in range(TILES):
                                act.wait_ge(scattered[t], 16 * (i - 1))
                        nc.scalar.copy(summed[0:n, b, :, :], sum_ps[b][0:n, :].rearrange(
                            "p (t d) -> p t d", t=TILES)).then_inc(summed_ready, 1)

                over_groups(act, group)

            both_ways(act, messages)

            for t in range(TILES):
                act.wait_ge(scattered[t], 16 * supers)

            def turned_nodes(m, b, j):
                n, s = number(m, b, j)
                act.wait_ge(nodes_turned, n + 1)
                if started(n - 1):
                    act.wait_ge(h1_done, n - 1)
                nc.scalar.copy(nodesT[:, s, :], nodesT_ps[s][:, 0:P]).then_inc(nodesT_ready, 1)

            def turned_hn(m, b, j):
                n, s = number(m, b, j)
                act.wait_ge(hn_turned, n + 1)
                if started(n - 1):
                    act.wait_ge(mlp_done, n - 1)
                for half in range(2):
                    nc.scalar.activation(reluT[:, s, half, :], hnT_ps[s][:, half * P:(half + 1) * P], ACT.Relu,
                                         scale=gamma_col[:, half:half + 1],
                                         bias=beta_col[:, half:half + 1]).then_inc(reluT_ready, 1)

            def first_std(m, b):
                act.wait_ge(mlp_mv, number(m, b)[0] + CHUNK)
                nc.scalar.activation(std[:, b, :], mv[:, b, :, 1], ACT.Sqrt, bias=ln_eps[:, 0:1]).then_inc(
                    mlp_std, 1)

            def second_std(m, b):
                act.wait_ge(ln2_mv, number(m, b)[0] + CHUNK)
                nc.scalar.activation(std2[:, :], mv2[:, :, 1], ACT.Sqrt, bias=ln_eps[:, 0:1]).then_inc(ln2_std, 1)

            def make_h2(m, b, j):
                n, _ = number(m, b, j)
                if j == 0:
                    act.wait_ge(ln2_nmr, 2 * m + b + 1)
                    if started(m):
                        act.wait_ge(h2_stored[b], 16 * m)
                nc.scalar.activation(h2_out[:, b, j * D:(j + 1) * D], X[:, bass.ds(n * D, D)],
                                     ACT.Relu, scale=rstd2[:, b, j:j + 1], bias=nmr2[:, b, j:j + 1]).then_inc(
                                         h2_ready, 1)

            def turn(*at):
                for node in lagging(at, TURN):
                    turned_nodes(*node)
                for node in lagging(at, SECOND - 1):
                    turned_hn(*node)
                for m, b, j in lagging(at, MOMENTS):
                    if j == CHUNK - 1:
                        first_std(m, b)
                for m, b, j in lagging(at, MOMENTS2):
                    if j == CHUNK - 1:
                        second_std(m, b)
                for node in lagging(at, H2):
                    make_h2(*node)

            half = aggT_words // 2
            nc.scalar.copy(aggT[:, half:], win_first[:, 0:1].to_broadcast([P, aggT_words - half])).then_inc(
                agg_zeroed, 1)
            turned_nodes(0, 0, 0)
            over_turns(turn)(act)

            for b in range(2):
                act.wait_ge(h2_stored[b], 16 * (chunks // 2))

            def index(c, n, i):
                nc.scalar.copy(gather_idx[0:n, c, :], src_col[0:n, cols(i)]).then_inc(gather_idx_ready, 1)

            def weigh(k, parts, following):
                for c, n in enumerate(parts):
                    i = SUPERS * k + c
                    act.wait_ge(gathered_landed[c], 16 * TILES * (k + 1))
                    if c < len(following):
                        index(c, following[c], i + SUPERS)
                    for t in range(TILES):
                        nc.scalar.activation(gathered[0:n, c, t, :], gathered[0:n, c, t, :], ACT.Copy,
                                             scale=w_col[0:n, bass.ds(TILES * i + t, 1)]).then_inc(weighted, 1)

            for c in range(SUPERS):
                index(c, P, c)
            nc.scalar.copy(deg, win_first[0:1, 0:1].to_broadcast([1, aggT_words])).then_inc(deg_zeroed, 1)
            with act.Fori(0, G - 1) as k:
                weigh(k, widths, widths)
            weigh(G - 1, widths, tail)
            weigh(G, tail, [])

            act.wait_ge(agg_added, 1)
            sums = aggT[:, 0:NP].rearrange("f (p j) -> f j p", j=NJ)

            def copies(m):
                for b in range(2):
                    q = 2 * m + b
                    if started(q - 1):
                        act.wait_ge(agg_turned, q - 1)
                    nc.scalar.copy(aggT_chunk[:, b, :, :], sums[:, bass.ds(q * CHUNK, CHUNK), :]).then_inc(
                        agg_copied, 1)

            over_chunks(act, copies)

        @block.vector
        def _(dve):
            done = [0]

            def prep_step(ins):
                ins.then_inc(prep, 1)
                done[0] += 1
                dve.wait_ge(prep, done[0])

            def by_super(rows):
                return rows.rearrange("p (c e) -> p c e", c=SUPERS)

            nc.vector.memset(X[96:P, (rest_nodes * D if full_parts == P - 1 else 0):], 0.0).then_inc(x_zeroed, 1)

            dve.wait_ge(idx_loaded, 16 * (3 * len(row_cuts) + 2))
            dve.wait_ge(const_ready, CONSTS)
            prep_step(nc.vector.tensor_copy(dst_f, dst_i))
            first = by_super(dst_f)[:, :, 0:1]
            prep_step(nc.vector.tensor_tensor(by_super(rel_f), by_super(dst_f),
                                              first.to_broadcast([P, SUPERS, SUPER]), ALU.subtract))
            dve.wait_ge(rel_cut, 1)
            prep_step(nc.vector.tensor_reduce(spread[:, 0:1], rel_f, AX_X, ALU.max))
            prep_step(nc.vector.tensor_reduce(spread[:, 1:2], rel_f, AX_X, ALU.min))
            prep_step(nc.vector.tensor_scalar(spread[:, 2:3], spread[:, 0:1], float(1 - WIN), None, ALU.add))
            prep_step(nc.vector.scalar_tensor_tensor(out=spread[:, 3:4], in0=spread[:, 1:2], scalar=-1.0,
                                                     in1=spread[:, 2:3], op0=ALU.mult, op1=ALU.max))
            assert done[0] == WAY_OUT_MADE
            dve.wait_ge(way_out_turned, 1)
            prep_step(nc.vector.tensor_reduce(spread[0:1, 0:1], bank[0][0:1, 0:P], AX_X, ALU.max))
            prep_step(nc.vector.tensor_scalar(flag_f[:, :], spread[0:1, 0:1], 0.0, None, ALU.is_le))
            assert done[0] == FLAG_MADE
            nc.vector.tensor_copy(flag_i[:, :], flag_f[:, :]).then_inc(flag_ready, 1)
            dve.wait_ge(flag_spread, 1)
            prep_step(nc.vector.tensor_copy(spread[:, 2:3], bank[1][:, 0:1]))
            prep_step(nc.vector.tensor_scalar(base_col[:, :], first.rearrange("p c a -> p (c a)"), spread[:, 2:3],
                                              None, ALU.mult))
            prep_step(nc.vector.tensor_tensor(
                by_super(rel_f), by_super(dst_f),
                base_col[:, :].rearrange("p (c a) -> p c a", a=1).to_broadcast([P, SUPERS, SUPER]), ALU.subtract))
            prep_step(nc.vector.tensor_copy(src_f, src_i))
            assert done[0] == ROWS_MADE
            prep_step(nc.vector.tensor_single_scalar(part_i, src_i, WIN - 1, op=ALU.bitwise_and))
            prep_step(nc.vector.tensor_tensor(src_hi, src_f, part_i, ALU.subtract))
            prep_step(nc.vector.tensor_copy(src_lo, part_i))
            prep_step(nc.vector.tensor_copy(dst_i, rel_f))
            prep_step(nc.vector.tensor_single_scalar(part_i, dst_i, WIN - 1, op=ALU.bitwise_and))
            prep_step(nc.vector.tensor_tensor(rel_hi, rel_f, part_i, ALU.subtract))
            prep_step(nc.vector.tensor_copy(rel_lo, part_i))
            assert done[0] == PARTS_MADE

            dve.wait_ge(weights_loaded, 16 * WEIGHTS)
            nc.vector.tensor_scalar(eps_col[:, :], eps_col[:, :], 1.0, None, ALU.add).then_inc(eps1_ready, 1)
            dve.wait_ge(x_loaded, 16 * len(node_cuts))

            def norm_x(m):
                for b in range(2):
                    q = 2 * m + b
                    for j in range(CHUNK):
                        nc.vector.bn_stats(stats[:, b, j, :], X[:, bass.ds((q * CHUNK + j) * D, D)]).then_inc(
                            ln_stats, 1)
                    dve.wait_ge(ln_stats, CHUNK * (q + 1))
                    dve.sem_inc(dve_turns, 1)
                    for j in range(CHUNK):
                        nc.vector.bn_aggr(mv[:, b, j, :], stats[:, b, j, :]).then_inc(ln_mv, 1)
                    if b or started(m):
                        scale_h(1 - b, q - 1, m if b else m - 1)
                    dve.wait_ge(ln_std, q + 1)
                    if started(m):
                        dve.wait_ge(h_made, q - 1)
                    nc.vector.reciprocal(rstd[:, b, :], std[:, b, :]).then_inc(ln_rstd, 1)
                    dve.wait_ge(ln_rstd, q + 1)
                    nc.vector.scalar_tensor_tensor(out=nmr[:, b, :], in0=mv[:, b, :, 0], scalar=-1.0,
                                                   in1=rstd[:, b, :], op0=ALU.mult, op1=ALU.mult).then_inc(ln_nmr, 1)

            def scale_h(b, q, m):
                dve.wait_ge(eps1_ready, 1)
                dve.wait_ge(h_made, q + 1)
                if started(m):
                    dve.wait_ge(eh_stored[b], 16 * m)
                nc.vector.tensor_scalar(eh_out[:, b, :], h_out[:, b, :], eps_col[:, 0:1], None,
                                        ALU.mult).then_inc(eh_ready, 1)

            over_chunks(dve, norm_x)
            scale_h(1, chunks - 1, chunks // 2 - 1)

            dve.wait_ge(flag_ready, 1)
            dve.wait_ge(col_ready, 3 * SUPERS)

            def messages(nw):
                def one_hot(c, n, i, step, w):
                    nc.vector.tensor_scalar(onehotT[0:WIN, c % 2, 0:n * TILES], dst_bc[c % 2][0:WIN, 0:n * TILES],
                                            win_node[0:WIN, bass.ds(w, 1)], None, ALU.is_equal).then_inc(
                                                onehotT_ready, 1)

                def merge_plan(c, n, i):
                    b = c % 2
                    dve.wait_ge(src_spread, i + 1)
                    if started(i - 1):
                        dve.wait_ge(merged, i - 1)
                    nc.vector.tensor_tensor(
                        same[0:n, b, :, 0:n],
                        src_bc[b][0:n, 0:n * TILES].rearrange("p (e t) -> p t e", t=TILES),
                        src_col[0:n, cols(i)].rearrange("p (t a) -> p t a", a=1).to_broadcast([n, TILES, n]),
                        ALU.is_equal).then_inc(same_ready, 1)
                    dve.wait_ge(same_ready, i + 1)
                    for t in range(TILES):
                        nc.vector.tensor_tensor_reduce(
                            out=masked[0:n, b, t, 0:n], in0=same[0:n, b, t, 0:n], in1=earlier[0:n, 0:n], scale=1.0,
                            scalar=0.0, op0=ALU.mult, op1=ALU.add,
                            accum_out=before[0:n, b, t:t + 1]).then_inc(before_ready, 1)
                    dve.wait_ge(before_ready, TILES * (i + 1))
                    nc.vector.tensor_scalar(dump_or_0[0:n, b, :], before[0:n, b, :], 1.0, dump_col[0:n, 0:1],
                                            ALU.min, ALU.mult).then_inc(dump_ready, 1)
                    dve.wait_ge(dump_ready, i + 1)
                    if started(i - 1):
                        dve.wait_ge(summed_ready, i - 1)
                    nc.vector.tensor_tensor(scatter_idx[0:n, c, :], dump_or_0[0:n, b, :], src_col[0:n, cols(i)],
                                            ALU.max).then_inc(scatter_idx_ready, 1)

                def add_h(c, n, k, i, step):
                    dve.wait_ge(ea_landed[c], 16 * (k + 1))
                    dve.wait_ge(h_gathered, step + 1)
                    if nw > 1 and started(step):
                        dve.wait_ge(h_added, step)
                    nc.vector.tensor_tensor(ea[0:n, c, :, :], ea[0:n, c, :, :], gath_ps[c % 2][0:n, :].rearrange(
                        "p (t d) -> p t d", t=TILES), ALU.add).then_inc(h_added, 1)

                def group(k, parts):
                    for c, n in enumerate(parts):
                        i = SUPERS * k + c
                        dve.wait_ge(dst_spread, i + 1)
                        if nw == 1:
                            one_hot(c, n, i, i, 0)
                            merge_plan(c, n, i)
                            add_h(c, n, k, i, i)
                        else:
                            merge_plan(c, n, i)
                            with dve.Fori(0, nw) as w:
                                one_hot(c, n, i, i * nw + w, w)
                                add_h(c, n, k, i, i * nw + w)

                over_groups(dve, group)

            both_ways(dve, messages)

            for t in range(TILES):
                dve.wait_ge(scattered[t], 16 * supers)

            dve.wait_ge(b2_added, chunks)
            nc.vector.memset(aggT[:, 0:aggT_words // 2], 0.0).then_inc(agg_zeroed, 1)

            def sum_first():
                dve.wait_ge(accs_landed[0], 16 * TILES)
                for t in (0, 2):
                    nc.vector.tensor_tensor(accs[:, 0, t, :], accs[:, 0, t, :], accs[:, 0, t + 1, :],
                                            ALU.add).then_inc(first_summed, 1)
                dve.wait_ge(first_summed, 2)
                nc.vector.tensor_tensor(nodes[:, 0, :], accs[:, 0, 0, :], accs[:, 0, 2, :], ALU.add).then_inc(
                    nodes_ready, 1)

            def first_product(m, b, j):
                n, s = number(m, b, j)
                dve.wait_ge(h1_done, n + 1)
                if started(n - 2 * CHUNK + 1):
                    dve.wait_ge(hn_turned, n - 2 * CHUNK + 1)
                nc.vector.tensor_tensor(h1[:, b, j, :], h1_ps[s][:, 0:H], b1_bc[:, :], ALU.add).then_inc(h1_ready, 1)

            def first_stats(m, b, j):
                dve.wait_ge(h1_ready, number(m, b, j)[0] + 1)
                nc.vector.bn_stats(stats[:, b, j, :], h1[:, b, j, :]).then_inc(mlp_stats, 1)

            def first_moments(m, b):
                dve.wait_ge(mlp_stats, number(m, b)[0] + CHUNK)
                dve.sem_inc(dve_turns, 1)
                for j in range(CHUNK):
                    nc.vector.bn_aggr(mv[:, b, j, :], stats[:, b, j, :]).then_inc(mlp_mv, 1)

            def first_norm(m, b):
                q = 2 * m + b
                dve.wait_ge(mlp_std, q + 1)
                nc.vector.reciprocal(rstd[:, b, :], std[:, b, :]).then_inc(mlp_rstd, 1)
                dve.wait_ge(mlp_rstd, q + 1)
                nc.vector.scalar_tensor_tensor(out=nmr[:, b, :], in0=mv[:, b, :, 0], scalar=-1.0,
                                               in1=rstd[:, b, :], op0=ALU.mult, op1=ALU.mult).then_inc(mlp_nmr, 1)

            def second_product(m, b, j):
                n, s = number(m, b, j)
                own = X[:, bass.ds(n * D, D)]
                dve.wait_ge(mlp_done, n + 1)
                nc.vector.tensor_tensor(own, own, mlp_ps[s][:, 0:D], ALU.add).then_inc(x1_ready, 1)

            def second_stats(m, b, j):
                n, _ = number(m, b, j)
                dve.wait_ge(x1_ready, n + 1)
                dve.sem_inc(dve_turns, 1)
                nc.vector.bn_stats(stats2[:, j, :], X[:, bass.ds(n * D, D)]).then_inc(ln2_stats, 1)

            def second_moments(m, b):
                dve.wait_ge(ln2_stats, number(m, b)[0] + CHUNK)
                dve.sem_inc(dve_turns, 1)
                for j in range(CHUNK):
                    nc.vector.bn_aggr(mv2[:, j, :], stats2[:, j, :]).then_inc(ln2_mv, 1)

            def second_norm(m, b):
                q = 2 * m + b
                dve.wait_ge(ln2_std, q + 1)
                if started(q - 1):
                    dve.wait_ge(h2_ready, number(m, b)[0] - CHUNK)
                nc.vector.reciprocal(rstd2[:, b, :], std2[:, :]).then_inc(ln2_rstd, 1)
                dve.wait_ge(ln2_rstd, q + 1)
                nc.vector.scalar_tensor_tensor(out=nmr2[:, b, :], in0=mv2[:, :, 0], scalar=-1.0,
                                               in1=rstd2[:, b, :], op0=ALU.mult, op1=ALU.mult).then_inc(ln2_nmr, 1)

            def turn(*at):
                first_whole = [(m, b) for m, b, j in lagging(at, MOMENTS) if j == CHUNK - 1]
                second_whole = [(m, b) for m, b, j in lagging(at, MOMENTS2) if j == CHUNK - 1]
                for chunk in first_whole:
                    first_moments(*chunk)
                for chunk in second_whole:
                    second_moments(*chunk)
                for node in lagging(at, 0):
                    first_product(*node)
                for node in lagging(at, SECOND):
                    second_product(*node)
                for chunk in first_whole:
                    first_norm(*chunk)
                for node in lagging(at, 0):
                    first_stats(*node)
                for node in lagging(at, SECOND):
                    second_stats(*node)
                for chunk in second_whole:
                    second_norm(*chunk)

            sum_first()
            over_turns(turn)(dve)

            for b in range(2):
                dve.wait_ge(h2_stored[b], 16 * (chunks // 2))
            dve.wait_ge(agg_zeroed, 2)
            dve.wait_ge(deg_zeroed, 1)

            def one_hot(b, n, rel):
                nc.vector.tensor_tensor(
                    onehot[0:n, b, :, :],
                    lane[0:n, :].rearrange("p (a v) -> p a v", a=1).to_broadcast([n, TILES, WIN]),
                    rel.rearrange("p (t a) -> p t a", a=1).to_broadcast([n, TILES, WIN]),
                    ALU.is_equal).then_inc(onehot_ready, 1)

            def add_sums(b, step, base):
                at = bass.ds(base, WIN)
                dve.wait_ge(agg_done, step + 1)
                if started(step):
                    dve.wait_ge(sums_added, 2 * step)
                nc.vector.tensor_tensor(aggT[:, at], aggT[:, at], agg_ps[b][:, 0:WIN], ALU.add).then_inc(
                    sums_added, 1)
                nc.vector.tensor_tensor(deg[:, at], deg[:, at], deg_ps[b][0:1, 0:WIN], ALU.add).then_inc(
                    sums_added, 1)

            def sums(nw):
                def group(k, parts):
                    for c, n in enumerate(parts):
                        i = SUPERS * k + c
                        if nw == 1:
                            if started(i - 1):
                                dve.wait_ge(agg_done, i - 1)
                            one_hot(c % 2, n, rel_col[0:n, cols(i)])
                            if started(i):
                                add_sums((c - 1) % 2, i - 1, dve.value_load(
                                    bases[0:1, bass.ds(i - 1, 1)], min_val=0, max_val=N - 1))
                        else:
                            with dve.Fori(0, nw) as w:
                                nc.vector.tensor_scalar(rel_win[0:n, :], rel_col[0:n, cols(i)],
                                                        win_first[0:n, bass.ds(w, 1)], None,
                                                        ALU.subtract).then_inc(rel_shifted, 1)
                                dve.wait_ge(rel_shifted, i * nw + w + 1)
                                one_hot(c % 2, n, rel_win[0:n, :])
                                add_sums(c % 2, i * nw + w, w * WIN)

                over_groups(dve, group)
                if nw == 1:
                    last = supers - 1
                    add_sums((len(tail) - 1) % 2, last, dve.value_load(
                        bases[0:1, last:last + 1], min_val=0, max_val=N - 1))
                dve.wait_ge(sums_added, 2 * supers * nw)

            both_ways(dve, sums)
            dve.sem_inc(agg_added, 1)

            def add_turned(m):
                for b in range(2):
                    q = 2 * m + b
                    dve.wait_ge(agg_turned, q + 1)
                    for j0, j1 in ((0, 4), (4, CHUNK)):
                        own = X[:, bass.ds((q * CHUNK + j0) * D, (j1 - j0) * D)]
                        nc.vector.tensor_tensor(own, own, bank[4 + 2 * b + j0 // 4][:, 0:(j1 - j0) * D],
                                                ALU.add).then_inc(agg_out, 1)

            def add_own(m):
                for b in range(2):
                    q = 2 * m + b
                    at = bass.ds(q * CHUNK * D, CHUNK * D)
                    dve.wait_ge(agg_out, 2 * (q + 1))
                    dve.wait_ge(own_ready, q + 1)
                    nc.vector.tensor_tensor(X[:, at], X[:, at], h2_in[:, at], ALU.add).then_inc(result_ready, 1)

            for m in range(2):
                add_turned(m)
            dve.wait_ge(deg_loaded, 16)
            nc.vector.tensor_scalar(no_edge[:, :], deg_nodes[:, :], 0.0, None, ALU.is_equal).then_inc(no_edge_ready, 1)
            with dve.Fori(2, chunks // 2) as m:
                add_own(m - 2)
                add_turned(m)
            for m in range(chunks // 2 - 2, chunks // 2):
                add_own(m)

_INS = ["x", "src", "dst", "edge_attr_128", "edge_weight", "L0_gnn_eps", "L0_gnn_W1", "L0_gnn_b1",
        "L0_gnn_gamma", "L0_gnn_beta", "L0_gnn_W2", "L0_gnn_b2"]


def kernel(**inputs):
    import numpy as _np
    import concourse.bacc as _bacc
    from concourse import mybir as _mybir
    from concourse.bass_utils import run_bass_kernel_spmd as _run

    nc = _bacc.Bacc("TRN2", target_bir_lowering=False, num_devices=1)
    arrays, args = {}, []
    for name in _INS:
        a = _np.ascontiguousarray(inputs[name])
        arrays[f"in_{name}"] = a
        args.append(nc.dram_tensor(f"in_{name}", a.shape, _mybir.dt.from_np(a.dtype), kind="ExternalInput").ap())
    shape = arrays["in_x"].shape
    args.append(nc.dram_tensor("out_0", shape, _mybir.dt.float32, kind="ExternalOutput").ap())
    build(nc, *args)
    r = _run(nc, [arrays], core_ids=[0])
    return r.results[0]["out_0"]
```
